# Optimizing a Trainium2 kernel written in Bass

```python
import numpy as np
import jax
import jax.numpy as jnp

def _softmax(x, axis=-1):
    return jax.nn.softmax(x, axis=axis)

def _gelu(x):
    return jax.nn.gelu(x, approximate=True)

def _silu(x):
    return jax.nn.silu(x)

def _sigmoid(x):
    return jax.nn.sigmoid(x)

def _layernorm(x, axis=-1, eps=1e-05):
    m = jnp.mean(x, axis=axis, keepdims=True)
    v = jnp.var(x, axis=axis, keepdims=True)
    return (x - m) / jnp.sqrt(v + eps)

def _scatter_add(tgt, idx, src, axis=0):
    return tgt.at[idx].add(src)

def _segment_sum(src, seg, n):
    return jax.ops.segment_sum(src, seg, n)
kernel_name = 'mk_dlrm_tower_d1_rec_r8_d4c152'

def setup_inputs(seed: int=0):
    np.random.seed(seed)
    _w = jnp.asarray

    def _rec_inputs():
        import jax
        import jax.numpy as jnp
        _tk = jax.random.key(seed)
        dense_ctx = jax.random.normal(jax.random.fold_in(_tk, 190), (2048, 16), jnp.float32)
        ids = jnp.stack([jax.random.randint(jax.random.fold_in(_tk, 200 + f), (2048,), 0, v, jnp.int32) for f, v in enumerate([1000, 12500, 1250, 1250, 1000, 12500, 1250, 125000, 1000, 1000, 125000, 12500, 125000, 1250, 125000, 1250, 1000, 125000, 1000, 12500, 1000, 1250, 12500, 1250, 1250, 1250, 125000, 1250, 1250, 125000, 1000, 1000, 1250, 12500, 1250, 1000, 1000, 1000, 1000])], axis=1)
        tbl_0 = 0.05 * jax.random.normal(jax.random.fold_in(_tk, 500 + 0), (1000, 32), jnp.float32)
        tbl_1 = 0.05 * jax.random.normal(jax.random.fold_in(_tk, 500 + 1), (12500, 32), jnp.float32)
        tbl_2 = 0.05 * jax.random.normal(jax.random.fold_in(_tk, 500 + 2), (1250, 32), jnp.float32)
        tbl_3 = 0.05 * jax.random.normal(jax.random.fold_in(_tk, 500 + 3), (1250, 32), jnp.float32)
        tbl_4 = 0.05 * jax.random.normal(jax.random.fold_in(_tk, 500 + 4), (1000, 32), jnp.float32)
        tbl_5 = 0.05 * jax.random.normal(jax.random.fold_in(_tk, 500 + 5), (12500, 32), jnp.float32)
        tbl_6 = 0.05 * jax.random.normal(jax.random.fold_in(_tk, 500 + 6), (1250, 32), jnp.float32)
        tbl_7 = 0.05 * jax.random.normal(jax.random.fold_in(_tk, 500 + 7), (125000, 32), jnp.float32)
        tbl_8 = 0.05 * jax.random.normal(jax.random.fold_in(_tk, 500 + 8), (1000, 32), jnp.float32)
        tbl_9 = 0.05 * jax.random.normal(jax.random.fold_in(_tk, 500 + 9), (1000, 32), jnp.float32)
        tbl_10 = 0.05 * jax.random.normal(jax.random.fold_in(_tk, 500 + 10), (125000, 32), jnp.float32)
        tbl_11 = 0.05 * jax.random.normal(jax.random.fold_in(_tk, 500 + 11), (12500, 32), jnp.float32)
        tbl_12 = 0.05 * jax.random.normal(jax.random.fold_in(_tk, 500 + 12), (125000, 32), jnp.float32)
        tbl_13 = 0.05 * jax.random.normal(jax.random.fold_in(_tk, 500 + 13), (1250, 32), jnp.float32)
        tbl_14 = 0.05 * jax.random.normal(jax.random.fold_in(_tk, 500 + 14), (125000, 32), jnp.float32)
        tbl_15 = 0.05 * jax.random.normal(jax.random.fold_in(_tk, 500 + 15), (1250, 32), jnp.float32)
        tbl_16 = 0.05 * jax.random.normal(jax.random.fold_in(_tk, 500 + 16), (1000, 32), jnp.float32)
        tbl_17 = 0.05 * jax.random.normal(jax.random.fold_in(_tk, 500 + 17), (125000, 32), jnp.float32)
        tbl_18 = 0.05 * jax.random.normal(jax.random.fold_in(_tk, 500 + 18), (1000, 32), jnp.float32)
        tbl_19 = 0.05 * jax.random.normal(jax.random.fold_in(_tk, 500 + 19), (12500, 32), jnp.float32)
        tbl_20 = 0.05 * jax.random.normal(jax.random.fold_in(_tk, 500 + 20), (1000, 32), jnp.float32)
        tbl_21 = 0.05 * jax.random.normal(jax.random.fold_in(_tk, 500 + 21), (1250, 32), jnp.float32)
        tbl_22 = 0.05 * jax.random.normal(jax.random.fold_in(_tk, 500 + 22), (12500, 32), jnp.float32)
        tbl_23 = 0.05 * jax.random.normal(jax.random.fold_in(_tk, 500 + 23), (1250, 32), jnp.float32)
        tbl_24 = 0.05 * jax.random.normal(jax.random.fold_in(_tk, 500 + 24), (1250, 32), jnp.float32)
        tbl_25 = 0.05 * jax.random.normal(jax.random.fold_in(_tk, 500 + 25), (1250, 32), jnp.float32)
        tbl_26 = 0.05 * jax.random.normal(jax.random.fold_in(_tk, 500 + 26), (125000, 32), jnp.float32)
        tbl_27 = 0.05 * jax.random.normal(jax.random.fold_in(_tk, 500 + 27), (1250, 32), jnp.float32)
        tbl_28 = 0.05 * jax.random.normal(jax.random.fold_in(_tk, 500 + 28), (1250, 32), jnp.float32)
        tbl_29 = 0.05 * jax.random.normal(jax.random.fold_in(_tk, 500 + 29), (125000, 32), jnp.float32)
        tbl_30 = 0.05 * jax.random.normal(jax.random.fold_in(_tk, 500 + 30), (1000, 32), jnp.float32)
        tbl_31 = 0.05 * jax.random.normal(jax.random.fold_in(_tk, 500 + 31), (1000, 32), jnp.float32)
        tbl_32 = 0.05 * jax.random.normal(jax.random.fold_in(_tk, 500 + 32), (1250, 32), jnp.float32)
        tbl_33 = 0.05 * jax.random.normal(jax.random.fold_in(_tk, 500 + 33), (12500, 32), jnp.float32)
        tbl_34 = 0.05 * jax.random.normal(jax.random.fold_in(_tk, 500 + 34), (1250, 32), jnp.float32)
        tbl_35 = 0.05 * jax.random.normal(jax.random.fold_in(_tk, 500 + 35), (1000, 32), jnp.float32)
        tbl_36 = 0.05 * jax.random.normal(jax.random.fold_in(_tk, 500 + 36), (1000, 32), jnp.float32)
        tbl_37 = 0.05 * jax.random.normal(jax.random.fold_in(_tk, 500 + 37), (1000, 32), jnp.float32)
        tbl_38 = 0.05 * jax.random.normal(jax.random.fold_in(_tk, 500 + 38), (1000, 32), jnp.float32)
        _rk = jax.random.fold_in(_tk, 7)
        W_top1 = 0.0693375 * jax.random.normal(jax.random.fold_in(_tk, 801), (208, 512), jnp.float32)
        W_top2 = 0.0441942 * jax.random.normal(jax.random.fold_in(_tk, 802), (512, 256), jnp.float32)
        W_top3 = 0.0625 * jax.random.normal(jax.random.fold_in(_tk, 803), (256, 1), jnp.float32)
        b_top1 = jnp.zeros((512,), jnp.float32)
        b_top2 = jnp.zeros((256,), jnp.float32)
        return (dense_ctx, ids, tbl_0, tbl_1, tbl_2, tbl_3, tbl_4, tbl_5, tbl_6, tbl_7, tbl_8, tbl_9, tbl_10, tbl_11, tbl_12, tbl_13, tbl_14, tbl_15, tbl_16, tbl_17, tbl_18, tbl_19, tbl_20, tbl_21, tbl_22, tbl_23, tbl_24, tbl_25, tbl_26, tbl_27, tbl_28, tbl_29, tbl_30, tbl_31, tbl_32, tbl_33, tbl_34, tbl_35, tbl_36, tbl_37, tbl_38, W_top1, b_top1, W_top2, b_top2, W_top3)
    dense_ctx, ids, tbl_0, tbl_1, tbl_2, tbl_3, tbl_4, tbl_5, tbl_6, tbl_7, tbl_8, tbl_9, tbl_10, tbl_11, tbl_12, tbl_13, tbl_14, tbl_15, tbl_16, tbl_17, tbl_18, tbl_19, tbl_20, tbl_21, tbl_22, tbl_23, tbl_24, tbl_25, tbl_26, tbl_27, tbl_28, tbl_29, tbl_30, tbl_31, tbl_32, tbl_33, tbl_34, tbl_35, tbl_36, tbl_37, tbl_38, W_top1, b_top1, W_top2, b_top2, W_top3 = _rec_inputs()

    def _L0_rec_setup():
        import jax, jax.numpy as jnp
        import numpy as np
        LAYER_SIZES = (128, 128)

        def _cin_layer(h0, h, W):
            F0, Fi = (h0.shape[1], h.shape[1])
            K = W.shape[1]
            Wr = W.reshape(F0, Fi, K)
            return jnp.einsum('bid,bjd,ijk->bkd', h0, h, Wr)
        key = jax.random.key(seed)
        k1, k2, k3 = jax.random.split(key, 3)
        B, F0, D = (256, 39, 32)
        F1 = LAYER_SIZES[0] // 2
        x = jax.random.normal(k1, (B, F0, D), dtype=jnp.float32)
        W1 = jax.random.normal(k2, (F0 * F0, LAYER_SIZES[0]), dtype=jnp.float32) * 0.05
        W2 = jax.random.normal(k3, (F0 * F1, LAYER_SIZES[1]), dtype=jnp.float32) * 0.05
        return {'x': x, 'W1': W1, 'W2': W2}
    _L0_rec_all = _L0_rec_setup()
    _L0_rec_in = {k: v for k, v in _L0_rec_all.items() if k in ('W1', 'W2')}
    del _L0_rec_all
    return {'dense_ctx': dense_ctx, 'ids': ids, 'tbl_0': tbl_0, 'tbl_1': tbl_1, 'tbl_2': tbl_2, 'tbl_3': tbl_3, 'tbl_4': tbl_4, 'tbl_5': tbl_5, 'tbl_6': tbl_6, 'tbl_7': tbl_7, 'tbl_8': tbl_8, 'tbl_9': tbl_9, 'tbl_10': tbl_10, 'tbl_11': tbl_11, 'tbl_12': tbl_12, 'tbl_13': tbl_13, 'tbl_14': tbl_14, 'tbl_15': tbl_15, 'tbl_16': tbl_16, 'tbl_17': tbl_17, 'tbl_18': tbl_18, 'tbl_19': tbl_19, 'tbl_20': tbl_20, 'tbl_21': tbl_21, 'tbl_22': tbl_22, 'tbl_23': tbl_23, 'tbl_24': tbl_24, 'tbl_25': tbl_25, 'tbl_26': tbl_26, 'tbl_27': tbl_27, 'tbl_28': tbl_28, 'tbl_29': tbl_29, 'tbl_30': tbl_30, 'tbl_31': tbl_31, 'tbl_32': tbl_32, 'tbl_33': tbl_33, 'tbl_34': tbl_34, 'tbl_35': tbl_35, 'tbl_36': tbl_36, 'tbl_37': tbl_37, 'tbl_38': tbl_38, 'W_top1': W_top1, 'b_top1': b_top1, 'W_top2': W_top2, 'b_top2': b_top2, 'W_top3': W_top3, 'L0_rec_W1': _L0_rec_in['W1'], 'L0_rec_W2': _L0_rec_in['W2']}

def reference(dense_ctx, ids, tbl_0, tbl_1, tbl_2, tbl_3, tbl_4, tbl_5, tbl_6, tbl_7, tbl_8, tbl_9, tbl_10, tbl_11, tbl_12, tbl_13, tbl_14, tbl_15, tbl_16, tbl_17, tbl_18, tbl_19, tbl_20, tbl_21, tbl_22, tbl_23, tbl_24, tbl_25, tbl_26, tbl_27, tbl_28, tbl_29, tbl_30, tbl_31, tbl_32, tbl_33, tbl_34, tbl_35, tbl_36, tbl_37, tbl_38, W_top1, b_top1, W_top2, b_top2, W_top3, L0_rec_W1, L0_rec_W2):
    import jax
    import jax.numpy as jnp

    def _L0_rec_ref(x, W1, W2):
        import jax, jax.numpy as jnp
        import numpy as np
        LAYER_SIZES = (128, 128)

        def _cin_layer(h0, h, W):
            F0, Fi = (h0.shape[1], h.shape[1])
            K = W.shape[1]
            Wr = W.reshape(F0, Fi, K)
            return jnp.einsum('bid,bjd,ijk->bkd', h0, h, Wr)
        conv1 = _cin_layer(x, x, W1)
        half = LAYER_SIZES[0] // 2
        hidden1 = conv1[:, :half, :]
        final1 = conv1[:, half:, :]
        conv2 = _cin_layer(x, hidden1, W2)
        final = jnp.concatenate([final1, conv2], axis=1)
        return jnp.sum(final, axis=2)
    e = jnp.stack([tbl_0[ids[:, 0]], tbl_1[ids[:, 1]], tbl_2[ids[:, 2]], tbl_3[ids[:, 3]], tbl_4[ids[:, 4]], tbl_5[ids[:, 5]], tbl_6[ids[:, 6]], tbl_7[ids[:, 7]], tbl_8[ids[:, 8]], tbl_9[ids[:, 9]], tbl_10[ids[:, 10]], tbl_11[ids[:, 11]], tbl_12[ids[:, 12]], tbl_13[ids[:, 13]], tbl_14[ids[:, 14]], tbl_15[ids[:, 15]], tbl_16[ids[:, 16]], tbl_17[ids[:, 17]], tbl_18[ids[:, 18]], tbl_19[ids[:, 19]], tbl_20[ids[:, 20]], tbl_21[ids[:, 21]], tbl_22[ids[:, 22]], tbl_23[ids[:, 23]], tbl_24[ids[:, 24]], tbl_25[ids[:, 25]], tbl_26[ids[:, 26]], tbl_27[ids[:, 27]], tbl_28[ids[:, 28]], tbl_29[ids[:, 29]], tbl_30[ids[:, 30]], tbl_31[ids[:, 31]], tbl_32[ids[:, 32]], tbl_33[ids[:, 33]], tbl_34[ids[:, 34]], tbl_35[ids[:, 35]], tbl_36[ids[:, 36]], tbl_37[ids[:, 37]], tbl_38[ids[:, 38]]], axis=1)
    z = _L0_rec_ref(e, L0_rec_W1, L0_rec_W2)
    z = z.reshape(z.shape[0], -1)
    h = jnp.concatenate([z, dense_ctx], axis=1)
    h = jnp.maximum(h @ W_top1 + b_top1, 0.0)
    h = jnp.maximum(h @ W_top2 + b_top2, 0.0)
    y = h @ W_top3
    return y

_drawn_inputs = setup_inputs


def setup_inputs(seed=0):
    import zlib

    import numpy as np

    out = dict(_drawn_inputs(seed))
    spreads = {'b_top1': (0.0, 0.1), 'b_top2': (0.0, 0.1)}
    factors = {'tbl_0': 4.813,
     'tbl_1': 4.709,
     'tbl_2': 4.95,
     'tbl_3': 4.926,
     'tbl_4': 4.826,
     'tbl_5': 4.445,
     'tbl_6': 4.769,
     'tbl_7': 4.637,
     'tbl_8': 4.919,
     'tbl_9': 4.91,
     'tbl_10': 4.9,
     'tbl_11': 4.507,
     'tbl_12': 4.739,
     'tbl_13': 4.59,
     'tbl_14': 4.453,
     'tbl_15': 4.79,
     'tbl_16': 4.532,
     'tbl_17': 4.63,
     'tbl_18': 4.834,
     'tbl_19': 5.021,
     'tbl_20': 5.027,
     'tbl_21': 4.94,
     'tbl_22': 5.033,
     'tbl_23': 4.94,
     'tbl_24': 4.678,
     'tbl_25': 4.731,
     'tbl_26': 4.774,
     'tbl_27': 4.642,
     'tbl_28': 4.66,
     'tbl_29': 4.789,
     'tbl_30': 4.231,
     'tbl_31': 4.747,
     'tbl_32': 5.007,
     'tbl_33': 4.437,
     'tbl_34': 4.958,
     'tbl_35': 4.781,
     'tbl_36': 5.106,
     'tbl_37': 4.747,
     'tbl_38': 4.639,
     'L0_rec_W2': 5.552}
    for name, (base, spread) in spreads.items():
        noise = np.random.default_rng([zlib.crc32(name.encode()), seed]).standard_normal(out[name].shape)
        drawn = base * np.exp(spread * noise) if base else spread * noise
        out[name] = jnp.asarray(drawn.astype(out[name].dtype))
    for name, factor in factors.items():
        out[name] = (out[name] * factor).astype(out[name].dtype)
    return out
```

```python
from contextlib import ExitStack

import concourse.bass as bass
from concourse import mybir

F32 = mybir.dt.float32
BF16 = mybir.dt.bfloat16
I32 = mybir.dt.int32
ALU = mybir.AluOpType
ACT = mybir.ActivationFunctionType

FIELDS = 39
DIM = 32
BATCH = 2048
TILE = 128
GROUPS = 4
BLOCKS = TILE // GROUPS
ROUNDS = BATCH // (2 * TILE)
QUARTERS = 4
QCOLS = TILE * DIM // QUARTERS
QBLOCKS = BLOCKS // QUARTERS
HALF = QCOLS // 2
HID = 64
FIN2 = 128
COPIES = 3
ROWS = COPIES * FIELDS
SHIFTS = (FIELDS + 1) // 2
CHUNKS = -(-SHIFTS // COPIES)
LAST_ROWS = (SHIFTS - COPIES * (CHUNKS - 1)) * FIELDS
HALF_F = (FIELDS + 1) // 2
PADDED = 2 * HALF_F
GCOLS = 2 * GROUPS * HALF_F
GRAM_BATCHES = (3, 3, 2)
RING = 4
TOP1, TOP2, CTX = 512, 256, 16
M1, M2 = TOP1 // 128, TOP2 // 128
PAIR = 2 * TILE
A_AT = 5
USES = CHUNKS + 1
SPREAD_AT = {False: {0: (0, 1), 1: (2,), 2: (3,), 3: (4,)}, True: {0: (0, 1, 2, 3, 4)}}
AUX_ROUND = 2 * (QUARTERS + QUARTERS * (1 + len(GRAM_BATCHES))) + 6
AUX_END = 1 + len(GRAM_BATCHES) + 6
Y_COPY = 2 * (1 + len(GRAM_BATCHES)) + 6
Y_LAST = AUX_END - QUARTERS


class Count:

    def __init__(self, start, n=0):
        self.start, self.n = start, n

    def next(self):
        self.n += 1
        return self.n

    def value(self, n=None):
        return self.start + (self.n if n is None else n)


def aux_start(i):
    return i * AUX_ROUND - (AUX_END - QUARTERS)


def product_rows(chunk):
    return LAST_ROWS if chunk == CHUNKS - 1 else ROWS


def uses_of_quarter():
    return [*range(A_AT), "left", *range(A_AT, CHUNKS)]


def dlrm_tower(nc, dense_t, ids, tables, w1_pairs, w1_mirrored, w1_final, w2_pairs,
               w_top1, b_top1, w_top2, b_top2, w_top3, selection, ident, y):
    ctx = ExitStack()
    with ctx:
        def sb(name, shape, dt=F32):
            return ctx.enter_context(nc.sbuf_tensor(name, shape, dt))

        def pb(name, shape, dt=F32):
            return ctx.enter_context(nc.psum_tensor(name, shape, dt))

        def sem(name):
            return ctx.enter_context(nc.semaphore(name))

        w_pair = sb("w_pair", [ROWS, CHUNKS, HID])
        w_mirror = sb("w_mirror", [ROWS, CHUNKS, HID])
        w_final = sb("w_final", [128, HALF_F, HID])
        w_second = sb("w_second", [128, HALF_F, FIN2])
        wt1_z1 = sb("wt1_z1", [128, TOP1])
        wt1_z2 = sb("wt1_z2", [128, TOP1])
        wt1_ctx = sb("wt1_ctx", [CTX, TOP1])
        wt2 = sb("wt2", [128, M1, TOP2])
        wt3 = sb("wt3", [128, M2])
        bias1 = sb("bias1", [128, M1])
        bias2 = sb("bias2", [128, M2])
        select = sb("select", [ROWS, 1 + CHUNKS, 128], BF16)
        eye_bf = sb("eye_bf", [128, 128], BF16)
        eye_f = sb("eye_f", [128, 128])
        ids_sb = [sb(f"ids_sb{p}", [TILE, FIELDS], I32) for p in range(2)]
        x_rows = [sb(f"x_rows{p}", [TILE, FIELDS * DIM]) for p in range(2)]
        x_gd = [sb(f"x_gd{p}", [128, PADDED, BLOCKS]) for p in range(2)]
        x_rest = sb("x_rest", [128, BLOCKS, FIELDS])
        x_parts = sb("x_parts", [128, BLOCKS, COPIES, FIELDS], BF16)
        x_cols = [sb(f"x_cols{p}", [ROWS, QUARTERS, QCOLS], BF16) for p in range(2)]
        left = [sb(f"left{q}", [ROWS, QCOLS]) for q in range(2)]
        product = [sb(f"product{r}", [ROWS, QCOLS]) for r in range(RING)]
        hidden = [sb(f"hidden{q}", [128, HALF]) for q in range(2)]
        hx = sb("hx", [128, BLOCKS, 2 * HID])
        x_diag = sb("x_diag", [128, BLOCKS, 2, GROUPS, HALF_F])
        gram_h = sb("gram_h", [128, HALF_F, PAIR])
        gram_x = sb("gram_x", [128, HALF_F, PAIR])
        z1 = sb("z1", [128, PAIR])
        z2 = sb("z2", [128, PAIR])
        ctx_t = sb("ctx_t", [CTX, PAIR])
        top1 = sb("top1", [128, M1, PAIR])
        top2 = sb("top2", [128, M2, PAIR])
        y_sb = sb("y_sb", [1, PAIR])

        selected_ps = [pb(f"selected_ps{s}", [128, QCOLS]) for s in range(2)]
        hidden_ps = [pb(f"hidden_ps{q}", [128, HALF]) for q in range(2)]
        aux_ps = [pb(f"aux_ps{n}", [128, HALF]) for n in range(2)]

        gathers_begun = sem("gathers_begun")
        consts = sem("consts_loaded")
        casts = sem("casts_loaded")
        ids_loaded = [sem(f"ids_loaded{p}") for p in range(2)]
        gathered = [sem(f"gathered{p}") for p in range(2)]
        ctx_loaded = sem("ctx_loaded")
        cleared = sem("buffers_cleared")
        weights_ready = sem("pair_weights_summed")
        x_turned = sem("x_turned")
        high_ready = sem("high_part_ready")
        rest_ready = sem("rest_ready")
        mid_ready = sem("mid_part_ready")
        parts_ready = sem("x_parts_ready")
        spread = sem("x_spread")
        selected = sem("selected")
        left_copied = sem("left_copied")
        products = sem("products_ready")
        summed = sem("products_summed")
        hidden_copied = sem("hidden_copied")
        aux_ready = sem("aux_ready")
        aux_copied = sem("aux_copied")
        y_free = sem("y_free")
        y_stored = sem("y_stored")

        CONSTS = [
            (w_pair[:], w1_pairs), (w_mirror[:], w1_mirrored), (eye_f[:], ident), (w_final[:], w1_final), (w_second[:], w2_pairs),
            (wt1_z1[0:HID, :], w_top1[0:HID, :]), (wt1_z1[HID:2 * HID, :], w_top1[0:HID, :]),
            (wt1_z2[:], w_top1[HID:HID + FIN2, :]), (wt1_ctx[:], w_top1[HID + FIN2:, :]),
            (wt2[:], w_top2.rearrange("(m p) n -> p m n", p=128)),
            (wt3[:], w_top3), (bias1[:], b_top1), (bias2[:], b_top2),
        ]

        CASTS = [(select[:], selection), (eye_bf[:], ident)]

        block = ctx.enter_context(nc.Block())

        @block.sync
        def _(sp):
            def load_ids(i, p):
                sp.dma_start(ids_sb[p][:], ids[bass.ds((2 * i + p) * TILE, TILE), :])\
                  .then_inc(ids_loaded[p], 16)

            def load_ctx(i):
                sp.dma_start(ctx_t[:], dense_t[:, bass.ds(i * PAIR, PAIR)]).then_inc(ctx_loaded, 16)

            def store_y(i):
                last = isinstance(i, int) and i == ROUNDS
                sp.wait_ge(aux_copied, aux_start(i) + (Y_LAST if last else Y_COPY))
                sp.dma_start(y[:, bass.ds((i - 1) * PAIR, PAIR)], y_sb[:]).then_inc(y_stored, 16)
                sp.wait_ge(y_stored, 16 * i)
                sp.sem_inc(y_free, 1)

            def next_ids(i):
                for p in range(2):
                    sp.wait_ge(gathered[p], 16 * FIELDS * i)
                    load_ids(i, p)

            def round_(i):
                store_y(i)
                load_ctx(i)

            for p in range(2):
                load_ids(0, p)
            for dst, src in CONSTS:
                sp.dma_start(dst, src).then_inc(consts, 16)
            load_ctx(0)
            next_ids(1)
            with sp.Fori(1, ROUNDS - 1) as i:
                next_ids(i + 1)
                round_(i)
            round_(ROUNDS - 1)
            store_y(ROUNDS)

        @block.gpsimd
        def _(pool):
            def gather(i, p, first):
                if not first:
                    pool.wait_ge(x_turned, 2 * i + p - 1)
                pool.wait_ge(ids_loaded[p], 16 * (i + 1))
                pool.sem_inc(gathers_begun, 1)
                for f in range(FIELDS):
                    pool.indirect_dma_start(
                        out=x_rows[p][:, f * DIM:(f + 1) * DIM], out_offset=None,
                        in_=tables[f], in_offset=bass.IndirectOffsetOnAxis(ap=ids_sb[p][:, f:f + 1], axis=0),
                    ).then_inc(gathered[p], 16)

            for dst, src in CASTS:
                pool.dma_start(dst, src).then_inc(casts, 16)
            for p in range(2):
                gather(0, p, True)
            with pool.Fori(1, ROUNDS) as i:
                for p in range(2):
                    gather(i, p, False)

        @block.vector
        def _(dve):
            def turn(i, p):
                dve.wait_ge(gathered[p], 16 * FIELDS * (i + 1))
                nc.vector.transpose(x_gd[p][:, 0:FIELDS, :].rearrange("p f l -> p (f l)"),
                                    x_rows[p][:]).then_inc(x_turned, 1)

            def rest(t, p):
                dve.wait_ge(high_ready, t + 1)
                nc.vector.tensor_tensor(x_rest[:], x_gd[p][:, 0:FIELDS, :].rearrange("p f l -> p l f"),
                                        x_parts[:, :, 0, :], ALU.subtract).then_inc(rest_ready, 1)

            def low(t):
                dve.wait_ge(mid_ready, t + 1)
                nc.vector.tensor_tensor(x_parts[:, :, 2, :], x_rest[:], x_parts[:, :, 1, :],
                                        ALU.subtract).then_inc(parts_ready, 1)

            def round_(i, first=False, last=False):
                sel = Count(2 * QUARTERS * USES * i + 1)
                prod = Count(2 * QUARTERS * CHUNKS * i)
                lefts = Count(2 * QUARTERS * i)
                for p in range(2):
                    more = not (last and p == 1)
                    i_next, p_next = (i, 1) if p == 0 else (i + 1, 0)
                    t_next = 2 * i + p + 1
                    for q in range(QUARTERS):
                        lefts.next()
                        for use in uses_of_quarter():
                            sel.next()
                            if use == "left":
                                continue
                            n = prod.next()
                            rows = product_rows(use)
                            if use == 0:
                                dve.wait_ge(left_copied, lefts.value())
                            skipped = int(not more and q == QUARTERS - 1 and use >= A_AT)
                            dve.wait_ge(selected, sel.value() - skipped)
                            if not first or n > RING:
                                dve.wait_ge(summed, prod.value() - RING)
                            nc.vector.tensor_tensor(
                                product[(n - 1) % RING][0:rows, :], left[q % 2][0:rows, :],
                                selected_ps[sel.n % 2][0:rows, :], ALU.mult).then_inc(products, 1)
                            if more and (q, use) == (0, 0):
                                if not (first and p == 0):
                                    dve.wait_ge(spread, t_next - 1)
                                turn(i_next, p_next)
                            if more and (q, use) == (0, 4):
                                rest(t_next, p_next)
                            if more and (q, use) == (1, 1):
                                low(t_next)

            for p in range(2):
                nc.vector.memset(x_gd[p][:, FIELDS:PADDED, :], 0.0).then_inc(cleared, 1)
            nc.vector.memset(hx[:, :, HID + FIELDS:2 * HID], 0.0).then_inc(cleared, 1)
            nc.vector.memset(x_diag[:].rearrange("p l a g f -> p (l a g f)"), 0.0).then_inc(cleared, 1)
            nc.vector.memset(y_sb[:], 0.0).then_inc(y_free, 1)
            dve.wait_ge(consts, 16 * len(CONSTS))
            nc.vector.tensor_tensor(w_pair[:], w_pair[:], w_mirror[:], ALU.add).then_inc(weights_ready, 1)
            turn(0, 0)
            rest(0, 0)
            low(0)
            round_(0, first=True)
            with dve.Fori(1, ROUNDS - 1) as i:
                round_(i)
            round_(ROUNDS - 1, last=True)

        @block.scalar
        def _(act):
            def copy(out, in_):
                return nc.scalar.activation(out, in_, ACT.Copy)

            def high(t, p):
                act.wait_ge(x_turned, t + 1)
                copy(x_parts[:, :, 0, :], x_gd[p][:, 0:FIELDS, :].rearrange("p f l -> p l f"))\
                    .then_inc(high_ready, 1)

            def mid(t):
                act.wait_ge(rest_ready, t + 1)
                copy(x_parts[:, :, 1, :], x_rest[:]).then_inc(mid_ready, 1)

            def spread_x(p, part):
                if part == 0:
                    copy(hx[:, :, HID:HID + FIELDS], x_gd[p][:, 0:FIELDS, :].rearrange("p f l -> p l f"))
                    return
                rows = slice(DIM * (part - 1), DIM * part)
                last = copy(x_diag[rows, :, :, part - 1, :],
                            x_gd[p][rows, :, :].rearrange("p (f a) l -> p l a f", a=2))
                if part == GROUPS:
                    last.then_inc(spread, 1)

            def take_left(sel, q, ahead=1):
                act.wait_ge(selected, sel.value(sel.n + ahead))
                copy(left[q % 2][:], selected_ps[(sel.n + ahead) % 2][0:ROWS, :]).then_inc(left_copied, 1)

            def take_hidden(n_summed, q):
                act.wait_ge(summed, n_summed)
                copy(hidden[q % 2][:], hidden_ps[q % 2][:]).then_inc(hidden_copied, 1)

            def aux(counts, work):
                n = counts.next()
                act.wait_ge(aux_ready, counts.value())
                work(aux_ps[(n - 1) % 2]).then_inc(aux_copied, 1)

            def x_turn(counts, p, q):
                aux(counts, lambda bank: copy(x_cols[p][:, q, :], bank[:].bitcast(BF16)[0:ROWS, :]))

            def hidden_turn(counts, q):
                out = hx[:, q * QBLOCKS:(q + 1) * QBLOCKS, 0:HID].rearrange("p (c m) k -> p m c k", c=2)
                aux(counts, lambda bank: copy(out, bank[:].rearrange("p (m c k) -> p m c k", c=2, k=HID)))

            def grams(counts, p, q, b):
                n = GRAM_BATCHES[b]
                l0 = q * QBLOCKS + sum(GRAM_BATCHES[:b])

                def work(bank):
                    view = bank[:, 0:n * GCOLS].rearrange("p (l a g f) -> p a l g f", a=2, g=GROUPS, f=HALF_F)
                    for to, rows in ((gram_h, 0), (gram_x, HID)):
                        cols = to[:, :, TILE * p:TILE * (p + 1)].rearrange("p f (g l) -> p l g f", g=GROUPS)
                        for a in range(2):
                            last = copy(cols[HID * a:HID * (a + 1), l0:l0 + n, :, :],
                                        view[rows:rows + HID, a, :, :, :])
                    return last

                aux(counts, work)

            def round_end(counts, step, i):
                def relu(out, bank, m0, bias, ms):
                    for k in range(ms):
                        last = nc.scalar.activation(out[:, m0 + k, :], bank[:, k * PAIR:(k + 1) * PAIR],
                                                    ACT.Relu, bias=bias[:, m0 + k:m0 + k + 1])
                    return last

                if step == "z":
                    aux(counts, lambda bank: copy(z2[:], bank[:, 0:PAIR]))
                    aux(counts, lambda bank: copy(z1[:], bank[:, 0:PAIR]))
                elif step == "top1":
                    aux(counts, lambda bank: relu(top1, bank, 0, bias1, 2))
                    aux(counts, lambda bank: relu(top1, bank, 2, bias1, 2))
                elif step == "top2":
                    aux(counts, lambda bank: relu(top2, bank, 0, bias2, 2))
                else:
                    act.wait_ge(y_free, i)
                    aux(counts, lambda bank: copy(y_sb[:], bank[0:1, 0:PAIR]))

            def quarter_end(counts, p, q):
                hidden_turn(counts, q)
                for b in range(len(GRAM_BATCHES)):
                    grams(counts, p, q, b)

            def round_(i, first=False, last=False):
                sel = Count(2 * QUARTERS * USES * i + 1)
                prod = Count(2 * QUARTERS * CHUNKS * i)
                aux_n = Count(QUARTERS if first else aux_start(i))
                for p in range(2):
                    more = not (last and p == 1)
                    i_next, p_next = (i, 1) if p == 0 else (i + 1, 0)
                    t = 2 * i + p
                    for q in range(QUARTERS):
                        before = (p, q - 1) if q else (1 - p, QUARTERS - 1)
                        has_before = not (first and (p, q) == (0, 0))
                        end_of_round = not first and (p, q) == (0, 1)
                        for pos, use in enumerate(uses_of_quarter()):
                            sel.next()
                            if pos == 0:
                                if has_before:
                                    take_hidden(prod.value(), before[1])
                            if q == 1:
                                for part in SPREAD_AT[end_of_round].get(pos, ()):
                                    spread_x(p, part)
                            if pos == 0 and end_of_round:
                                round_end(aux_n, "z", i)
                            if pos == 1 and q >= 2 and more:
                                x_turn(aux_n, p_next, 2 * (q - 2))
                            if pos == 2 and q >= 2 and more:
                                x_turn(aux_n, p_next, 2 * (q - 2) + 1)
                            if pos == 2 and q == 0 and more:
                                high(t + 1, p_next)
                            if pos == 3:
                                if has_before:
                                    hidden_turn(aux_n, before[1])
                                if end_of_round:
                                    round_end(aux_n, "top1", i)
                            if pos == 4 and (more or q < QUARTERS - 1):
                                take_left(sel, q + 1)
                            if pos == 4 and has_before:
                                grams(aux_n, *before, 0)
                            if pos == 6:
                                if has_before:
                                    grams(aux_n, *before, 1)
                                if end_of_round:
                                    round_end(aux_n, "top2", i)
                            if pos == 7:
                                if q == 0 and more:
                                    mid(t + 1)
                                if has_before:
                                    grams(aux_n, *before, 2)
                                if end_of_round:
                                    round_end(aux_n, "y", i)
                            if use != "left":
                                prod.next()
                return aux_n

            act.wait_ge(cleared, 4)
            act.wait_ge(consts, 16 * len(CONSTS))
            high(0, 0)
            mid(0)
            aux_n = Count(0)
            for q in range(QUARTERS):
                x_turn(aux_n, 0, q)
                if q == 0:
                    take_left(Count(1), 0, ahead=0)
            round_(0, first=True)
            with act.Fori(1, ROUNDS - 1) as i:
                round_(i)
            aux_n = round_(ROUNDS - 1, last=True)
            take_hidden(2 * QUARTERS * CHUNKS * ROUNDS, QUARTERS - 1)
            quarter_end(aux_n, 1, QUARTERS - 1)
            for step in ("z", "top1", "top2", "y"):
                round_end(aux_n, step, ROUNDS)

        @block.tensor
        def _(pe):
            def aux(counts, work, needs=None):
                n = counts.next()
                least = n - 2 if needs is None else max(n - 2, needs)
                if not isinstance(counts.start, int) or counts.start + least > 0:
                    pe.wait_ge(aux_copied, counts.value(least))
                work(aux_ps[(n - 1) % 2]).then_inc(aux_ready, 1)
                return n

            def x_turn(counts, t, p, q):
                if q == 0:
                    pe.wait_ge(parts_ready, t + 1)

                def work(bank):
                    for m in range(QBLOCKS):
                        last = nc.tensor.transpose(
                            bank[:].bitcast(BF16)[0:ROWS, m * 128:(m + 1) * 128],
                            x_parts[:, q * QBLOCKS + m, :, :].rearrange("p c f -> p (c f)"), eye_bf[:])
                    return last

                aux(counts, work)

            def hidden_turn(counts, n_copied, q):
                pe.wait_ge(hidden_copied, n_copied)

                def work(bank):
                    for m in range(HALF // 128):
                        cols = slice(m * 128, (m + 1) * 128)
                        last = nc.tensor.transpose(bank[:, cols], hidden[q % 2][:, cols], eye_f[:])
                    return last

                return aux(counts, work)

            def grams(counts, turned, n_spread, q, b):
                if b == 0:
                    pe.wait_ge(spread, n_spread)
                l0 = q * QBLOCKS + sum(GRAM_BATCHES[:b])

                def work(bank):
                    for m in range(GRAM_BATCHES[b]):
                        last = nc.tensor.matmul(
                            bank[:, m * GCOLS:(m + 1) * GCOLS], hx[:, l0 + m, :],
                            x_diag[:, l0 + m, :, :, :].rearrange("p a g f -> p (a g f)"),
                            start=True, stop=True)
                    return last

                return aux(counts, work, turned)

            def z_step(counts, needs):
                def second(bank):
                    for f in range(HALF_F):
                        last = nc.tensor.matmul(bank[:, 0:PAIR], w_second[:, f, :], gram_h[:, f, :],
                                                start=f == 0, stop=f == HALF_F - 1)
                    return last

                def first_(bank):
                    for f in range(HALF_F):
                        half = f % 2
                        last = nc.tensor.matmul(bank[HID * half:HID * (half + 1), 0:PAIR],
                                                w_final[:, f, :], gram_x[:, f, :],
                                                start=f < 2, stop=f >= HALF_F - 2)
                    return last

                aux(counts, second, needs)
                return aux(counts, first_, needs)

            def top1_step(counts, needs, i):
                pe.wait_ge(ctx_loaded, 16 * i)
                for h in range(2):
                    def work(bank):
                        for k in range(2):
                            cols = slice((2 * h + k) * 128, (2 * h + k + 1) * 128)
                            out = bank[:, k * PAIR:(k + 1) * PAIR]
                            nc.tensor.matmul(out, wt1_z1[:, cols], z1[:], start=True, stop=False)
                            nc.tensor.matmul(out, wt1_z2[:, cols], z2[:], start=False, stop=False)
                            last = nc.tensor.matmul(out, wt1_ctx[:, cols], ctx_t[:], start=False, stop=True)
                        return last
                    n = aux(counts, work, needs)
                return n

            def top2_step(counts, needs):
                def work(bank):
                    for k in range(M2):
                        out = bank[:, k * PAIR:(k + 1) * PAIR]
                        for m in range(M1):
                            last = nc.tensor.matmul(out, wt2[:, m, k * 128:(k + 1) * 128], top1[:, m, :],
                                                    start=m == 0, stop=m == M1 - 1)
                    return last
                return aux(counts, work, needs)

            def y_step(counts, needs):
                def work(bank):
                    for m in range(M2):
                        last = nc.tensor.matmul(bank[0:1, 0:PAIR], wt3[:, m:m + 1], top2[:, m, :],
                                                start=m == 0, stop=m == M2 - 1)
                    return last
                aux(counts, work, needs)

            def select_into(n_selected, what, p, q):
                chunk = 0 if what == "left" else 1 + what
                for h in range(2):
                    last = nc.tensor.matmul(selected_ps[n_selected % 2][:, h * HALF:(h + 1) * HALF],
                                            select[:, chunk, :], x_cols[p][:, q, h * HALF:(h + 1) * HALF],
                                            start=True, stop=True)
                last.then_inc(selected, 1)

            def sum_products(n, chunk, q):
                rows = product_rows(chunk)
                for c in range(2):
                    last = nc.tensor.matmul(hidden_ps[q % 2][HID * c:HID * (c + 1), :],
                                            w_pair[0:rows, chunk, :],
                                            product[(n - 1) % RING][0:rows, c * HALF:(c + 1) * HALF],
                                            start=chunk == 0, stop=chunk == CHUNKS - 1)
                last.then_inc(summed, 1)

            def round_(i, first=False, last=False):
                sel = Count(2 * QUARTERS * USES * i + 1)
                prod = Count(2 * QUARTERS * CHUNKS * i)
                lefts = Count(2 * QUARTERS * i + 1)
                hid = Count(2 * QUARTERS * i)
                aux_n = Count(QUARTERS if first else aux_start(i))
                order = [(p, q, use) for p in range(2) for q in range(QUARTERS) for use in uses_of_quarter()]
                order += [(2, 0, 0), (2, 0, 1)]
                for n_use, (p, q, use) in enumerate(order[:-2]):
                    pos = n_use % USES
                    more = not (last and p == 1)
                    t = 2 * i + p
                    before = (p, q - 1) if q else (1 - p, QUARTERS - 1)
                    has_before = not (first and (p, q) == (0, 0))
                    end_of_round = not first and (p, q) == (0, 1)
                    if use == "left":
                        lefts.next()
                        if more or q < QUARTERS - 1:
                            pe.wait_ge(left_copied, lefts.value())
                    else:
                        n = prod.next()
                        pe.wait_ge(products, prod.value())
                    p2, q2, use2 = order[n_use + 2]
                    if use2 == "left":
                        q2 += 1
                    p2, q2 = p2 + q2 // QUARTERS, q2 % QUARTERS
                    if not (last and p2 == 2):
                        if (q2, use2) in ((0, "left"), (1, "left"), (2, "left"), (3, "left")):
                            if q2 == 0:
                                pe.wait_ge(aux_copied, aux_n.value(x_turned_n))
                        select_into(sel.n + 2 + 1, use2, p2 % 2, q2)
                    sel.next()
                    if use != "left":
                        if use == 0 and (not first or p or q >= 2):
                            pe.wait_ge(hidden_copied, hid.value() - 1)
                        sum_products(n, use, q)
                    if pos == 0 and end_of_round:
                        z_n = z_step(aux_n, gram_n)
                    if pos in (0, 1) and q >= 2 and more:
                        x_turn(aux_n, t + 1, 1 - p, 2 * (q - 2) + pos)
                        x_turned_n = aux_n.n
                    if pos == 2:
                        if has_before:
                            turned_n = hidden_turn(aux_n, hid.value(), before[1])
                        if end_of_round:
                            top_n = top1_step(aux_n, z_n, i)
                    if has_before and pos in (4, 6, 7):
                        b = (4, 6, 7).index(pos)
                        n_spread = t + 1 if q else t
                        gram_n = grams(aux_n, turned_n, n_spread, before[1], b)
                    if end_of_round and pos == 6:
                        top_n = top2_step(aux_n, top_n)
                    if end_of_round and pos == 7:
                        y_step(aux_n, top_n)
                    if pos == USES - 1:
                        hid.next()
                return aux_n

            pe.wait_ge(consts, 16 * len(CONSTS))
            pe.wait_ge(casts, 16 * len(CASTS))
            pe.wait_ge(cleared, 4)
            pe.wait_ge(weights_ready, 1)
            aux_n = Count(0)
            for q in range(QUARTERS):
                x_turn(aux_n, 0, 0, q)
                if q == 0:
                    pe.wait_ge(aux_copied, 1)
                    select_into(0, "left", 0, 0)
                    select_into(1, 0, 0, 0)
            pe.wait_ge(aux_copied, QUARTERS)
            pe.wait_ge(left_copied, 1)
            select_into(2, 1, 0, 0)
            round_(0, first=True)
            with pe.Fori(1, ROUNDS - 1) as i:
                round_(i)
            aux_n = round_(ROUNDS - 1, last=True)
            turned_n = hidden_turn(aux_n, 2 * QUARTERS * ROUNDS, QUARTERS - 1)
            for b in range(len(GRAM_BATCHES)):
                gram_n = grams(aux_n, turned_n, 2 * ROUNDS, QUARTERS - 1, b)
            z_n = z_step(aux_n, gram_n)
            top_n = top1_step(aux_n, z_n, ROUNDS)
            top_n = top2_step(aux_n, top_n)
            y_step(aux_n, top_n)


def build(nc, a, out):
    dlrm_tower(nc, a["dense_t"], a["ids"], [a[f"tbl_{f}"] for f in range(FIELDS)], a["w1_pairs"],
               a["w1_mirrored"], a["w1_final"], a["w2_pairs"], a["w_top1"], a["b_top1"], a["w_top2"],
               a["b_top2"], a["w_top3"], a["selection"], a["ident"], out)


def lay_out(inputs):
    import numpy as np

    w1 = np.asarray(inputs["L0_rec_W1"]).reshape(FIELDS, FIELDS, 2 * HID)
    w2 = np.asarray(inputs["L0_rec_W2"]).reshape(FIELDS, HID, FIN2)
    i = np.arange(FIELDS)
    pairs = np.zeros((COPIES, FIELDS, CHUNKS, HID), np.float32)
    mirrored = np.zeros((COPIES, FIELDS, CHUNKS, HID), np.float32)
    selection = np.zeros((COPIES, FIELDS, 1 + CHUNKS, 128), np.float32)
    for a in range(COPIES):
        selection[:, i, 0, a * FIELDS + i] = 1.0
        for c in range(CHUNKS):
            shift = COPIES * c + a
            if shift >= SHIFTS:
                continue
            j = (i + shift) % FIELDS
            pairs[a, :, c] = w1[i, j, :HID]
            if shift:
                mirrored[a, :, c] = w1[j, i, :HID]
            selection[:, j, 1 + c, a * FIELDS + i] = 1.0
    final = np.zeros((HALF_F, 2, HID, HID), np.float32)
    second = np.zeros((HALF_F, 2, HID, FIN2), np.float32)
    for f in range(FIELDS):
        final[f // 2, f % 2, :FIELDS] = w1[:, f, HID:]
        second[f // 2, f % 2] = w2[f]
    arrays = {
        "dense_t": np.asarray(inputs["dense_ctx"]).T,
        "ids": np.asarray(inputs["ids"]),
        "w1_pairs": pairs.reshape(ROWS, CHUNKS, HID),
        "w1_mirrored": mirrored.reshape(ROWS, CHUNKS, HID),
        "w1_final": final.transpose(1, 2, 0, 3).reshape(128, HALF_F, HID),
        "w2_pairs": second.transpose(1, 2, 0, 3).reshape(128, HALF_F, FIN2),
        "w_top1": np.asarray(inputs["W_top1"]),
        "b_top1": np.asarray(inputs["b_top1"]).reshape(M1, 128).T,
        "w_top2": np.asarray(inputs["W_top2"]),
        "b_top2": np.asarray(inputs["b_top2"]).reshape(M2, 128).T,
        "w_top3": np.asarray(inputs["W_top3"]).reshape(M2, 128).T,
        "selection": selection.reshape(ROWS, 1 + CHUNKS, 128),
        "ident": np.eye(128, dtype=np.float32),
    }
    for f in range(FIELDS):
        arrays[f"tbl_{f}"] = np.asarray(inputs[f"tbl_{f}"])
    return {k: np.ascontiguousarray(v) for k, v in arrays.items()}


def kernel(**inputs):
    import concourse.bacc as bacc
    from concourse.bass_utils import run_bass_kernel_spmd

    arrays = lay_out(inputs)
    nc = bacc.Bacc("TRN2", target_bir_lowering=False, num_devices=1)
    args = {}
    for name, v in arrays.items():
        args[name] = nc.dram_tensor(f"in_{name}", v.shape, mybir.dt.from_np(v.dtype), kind="ExternalInput").ap()
    out = nc.dram_tensor("y_out", (1, BATCH), F32, kind="ExternalOutput").ap()
    build(nc, args, out)
    r = run_bass_kernel_spmd(nc, [{f"in_{k}": v for k, v in arrays.items()}], core_ids=[0])
    return r.results[0]["y_out"].reshape(BATCH, 1)
```

```python
from contextlib import ExitStack

import concourse.bass as bass
from concourse import mybir

F32 = mybir.dt.float32
BF16 = mybir.dt.bfloat16
I32 = mybir.dt.int32
ALU = mybir.AluOpType
ACT = mybir.ActivationFunctionType

FIELDS = 39
DIM = 32
BATCH = 2048
TILE = 128
GROUPS = 4
BLOCKS = TILE // GROUPS
ROUNDS = BATCH // (2 * TILE)
QUARTERS = 4
QCOLS = TILE * DIM // QUARTERS
QBLOCKS = BLOCKS // QUARTERS
HALF = QCOLS // 2
HID = 64
FIN2 = 128
COPIES = 3
ROWS = COPIES * FIELDS
SHIFTS = (FIELDS + 1) // 2
CHUNKS = -(-SHIFTS // COPIES)
LAST_ROWS = (SHIFTS - COPIES * (CHUNKS - 1)) * FIELDS
HALF_F = (FIELDS + 1) // 2
PADDED = 2 * HALF_F
GCOLS = 2 * GROUPS * HALF_F
GRAM_BATCHES = (3, 3, 2)
SELECTED = 3
TOP1, TOP2, CTX = 512, 256, 16
M1, M2 = TOP1 // 128, TOP2 // 128
PAIR = 2 * TILE
USES = SELECTED + 1
ORDER = (0, 1, 3, 2, 4, 5, 6)
BANK = {0: 0, 1: 1, 2: 0, "left": 1}
SELECT_AT = {0: (2, 0), 1: ("left", 1), 3: (0, 1), 4: (1, 1)}
LEFT_AT = 1
PREPARE = {"turn": (1, 4), "high": (1, 5), "rest": (2, 0), "mid": (2, 1), "low": (2, 3)}
TURN_SECOND = (3, 3)
COLS_AT = {(2, 4): 0, (2, 6): 1, (3, 0): 2, (3, 3): 3}
ALL = slice(0, BLOCKS)
AHEAD, OTHERS = slice(0, QBLOCKS), slice(QBLOCKS, BLOCKS)
STARTED = 2
GRAM_AT = (4, 5, 6)
SPREAD_AT = {False: {0: (0, 1), 1: (2, 3), 2: (4,)}, True: {0: (0, 1, 2, 3, 4)}}
AUX_ROUND = 2 * (QUARTERS + QUARTERS * (1 + len(GRAM_BATCHES))) + 6
AUX_END = 1 + len(GRAM_BATCHES) + 6
Y_COPY = 2 * (1 + len(GRAM_BATCHES)) + 6
Y_LAST = AUX_END - QUARTERS


class Count:

    def __init__(self, start, n=0):
        self.start, self.n = start, n

    def next(self):
        self.n += 1
        return self.n

    def value(self, n=None):
        return self.start + (self.n if n is None else n)


def aux_start(i):
    return i * AUX_ROUND - (AUX_END - QUARTERS)


def product_rows(chunk):
    return LAST_ROWS if chunk == CHUNKS - 1 else ROWS


def is_shifted(chunk):
    return chunk >= SELECTED


def dlrm_tower(nc, dense_t, ids, tables, w1_pairs, w1_mirrored, w1_final, w2_pairs,
               w_top1, b_top1, w_top2, b_top2, w_top3, selection, ident, y):
    ctx = ExitStack()
    with ctx:
        def sb(name, shape, dt=F32):
            return ctx.enter_context(nc.sbuf_tensor(name, shape, dt))

        def pb(name, shape, dt=F32):
            return ctx.enter_context(nc.psum_tensor(name, shape, dt))

        def sem(name):
            return ctx.enter_context(nc.semaphore(name))

        w_pair = sb("w_pair", [ROWS, CHUNKS, HID])
        w_final = sb("w_final", [128, HALF_F, HID])
        w_second = sb("w_second", [128, HALF_F, FIN2])
        wt1_z1 = sb("wt1_z1", [128, TOP1])
        wt1_z2 = sb("wt1_z2", [128, TOP1])
        wt1_ctx = sb("wt1_ctx", [CTX, TOP1])
        wt2 = sb("wt2", [128, M1, TOP2])
        wt3 = sb("wt3", [128, M2])
        bias1 = sb("bias1", [128, M1])
        bias2 = sb("bias2", [128, M2])
        select = sb("select", [ROWS, 1 + CHUNKS, 128], BF16)
        eye_bf = sb("eye_bf", [128, 128], BF16)
        eye_f = sb("eye_f", [128, 128])
        ids_sb = [sb(f"ids_sb{p}", [TILE, FIELDS], I32) for p in range(2)]
        x_rows = [sb(f"x_rows{p}", [TILE, FIELDS * DIM]) for p in range(2)]
        x_gd = [sb(f"x_gd{p}", [128, PADDED, BLOCKS]) for p in range(2)]
        x_rest = sb("x_rest", [128, BLOCKS, FIELDS])
        x_parts = sb("x_parts", [128, BLOCKS, COPIES, FIELDS], BF16)
        x_cols = [sb(f"x_cols{p}", [ROWS, QUARTERS, QCOLS], BF16) for p in range(2)]
        left = [sb(f"left{q}", [ROWS, QCOLS]) for q in range(2)]
        product = [sb(f"product{c}", [ROWS, QCOLS]) for c in range(CHUNKS)]
        select_f = product[CHUNKS - 2][:].rearrange("r (c n) -> r c n", n=128)
        w_mirror = product[CHUNKS - 1][:, 0:CHUNKS * HID].rearrange("r (c k) -> r c k", k=HID)
        hidden = [sb(f"hidden{q}", [128, HALF]) for q in range(2)]
        hx = sb("hx", [128, BLOCKS, 2 * HID])
        x_diag = sb("x_diag", [128, BLOCKS, 2, GROUPS, HALF_F])
        gram_h = sb("gram_h", [128, HALF_F, PAIR])
        gram_x = sb("gram_x", [128, HALF_F, PAIR])
        z1 = sb("z1", [128, PAIR])
        z2 = sb("z2", [128, PAIR])
        ctx_t = sb("ctx_t", [CTX, PAIR])
        top1 = sb("top1", [128, M1, PAIR])
        top2 = sb("top2", [128, M2, PAIR])
        y_sb = sb("y_sb", [1, PAIR])

        selected_ps = [pb(f"selected_ps{s}", [128, QCOLS]) for s in range(2)]
        hidden_ps = [pb(f"hidden_ps{q}", [128, HALF]) for q in range(2)]
        aux_ps = [pb(f"aux_ps{n}", [128, HALF]) for n in range(2)]

        gathers_begun = sem("gathers_begun")
        consts = sem("consts_loaded")
        cast = sem("constants_cast")
        ids_loaded = [sem(f"ids_loaded{p}") for p in range(2)]
        gathered = [sem(f"gathered{p}") for p in range(2)]
        ctx_loaded = sem("ctx_loaded")
        cleared = sem("buffers_cleared")
        weights_ready = sem("pair_weights_summed")
        x_turned = sem("x_turned")
        high_ready = sem("high_part_ready")
        rest_ready = sem("rest_ready")
        mid_ready = sem("mid_part_ready")
        parts_ready = sem("x_parts_ready")
        spread = sem("x_spread")
        selected = sem("selected")
        left_copied = sem("left_copied")
        shifted = {c: sem(f"chunk{c}_shifted") for c in range(CHUNKS) if is_shifted(c)}
        products = sem("products_ready")
        summed = sem("products_summed")
        hidden_copied = sem("hidden_copied")
        aux_ready = sem("aux_ready")
        aux_copied = sem("aux_copied")
        y_free = sem("y_free")
        y_stored = sem("y_stored")

        CONSTS = [
            (w_pair[:], w1_pairs), (w_mirror, w1_mirrored), (eye_f[:], ident), (select_f, selection),
            (w_final[:], w1_final), (w_second[:], w2_pairs),
            (wt1_z1[0:HID, :], w_top1[0:HID, :]), (wt1_z1[HID:2 * HID, :], w_top1[0:HID, :]),
            (wt1_z2[:], w_top1[HID:HID + FIN2, :]), (wt1_ctx[:], w_top1[HID + FIN2:, :]),
            (wt2[:], w_top2.rearrange("(m p) n -> p m n", p=128)),
            (wt3[:], w_top3), (bias1[:], b_top1), (bias2[:], b_top2),
        ]

        block = ctx.enter_context(nc.Block())

        @block.sync
        def _(sp):
            def load_ids(i, p):
                sp.dma_start(ids_sb[p][:], ids[bass.ds((2 * i + p) * TILE, TILE), :])\
                  .then_inc(ids_loaded[p], 16)

            def load_ctx(i):
                sp.dma_start(ctx_t[:], dense_t[:, bass.ds(i * PAIR, PAIR)]).then_inc(ctx_loaded, 16)

            def store_y(i):
                last = isinstance(i, int) and i == ROUNDS
                sp.wait_ge(aux_copied, aux_start(i) + (Y_LAST if last else Y_COPY))
                sp.dma_start(y[:, bass.ds((i - 1) * PAIR, PAIR)], y_sb[:]).then_inc(y_stored, 16)
                sp.wait_ge(y_stored, 16 * i)
                sp.sem_inc(y_free, 1)

            def next_ids(i, p):
                sp.wait_ge(gathered[p], 16 * FIELDS * i)
                load_ids(i, p)

            def shift_right_factors(n_quarter, left_q):
                for c in shifted:
                    step = ORDER.index(c)
                    if c == SELECTED:
                        sp.wait_ge(left_copied, n_quarter + 1)
                    if isinstance(n_quarter, int) and n_quarter == 0:
                        sp.wait_ge(weights_ready, 1)
                        sp.wait_ge(cast, 2)
                    else:
                        sp.wait_ge(summed, CHUNKS * n_quarter - CHUNKS + step + 1)
                    copies = product_rows(c) // FIELDS
                    for a in range(copies):
                        shift = COPIES * c + a
                        sp.dma_start(product[c][a * FIELDS:(a + 1) * FIELDS, :],
                                     left[left_q][shift:shift + FIELDS, :]).then_inc(shifted[c], 16)

            def round_(i, first=False, last=False):
                for n in range(2 * QUARTERS):
                    if n % QUARTERS == 0 and not last:
                        next_ids(i + 1, n // QUARTERS)
                    if n == 2 and not first:
                        store_y(i)
                        load_ctx(i)
                    if not (last and n == 2 * QUARTERS - 1):
                        shift_right_factors(2 * QUARTERS * i + n + 1, (n + 1) % 2)

            for p in range(2):
                load_ids(0, p)
            for dst, src in CONSTS:
                sp.dma_start(dst, src).then_inc(consts, 16)
            load_ctx(0)
            shift_right_factors(0, 0)
            round_(0, first=True)
            with sp.Fori(1, ROUNDS - 1) as i:
                round_(i)
            round_(ROUNDS - 1, last=True)
            store_y(ROUNDS)

        @block.gpsimd
        def _(pool):
            def gather(i, p, first):
                if not first:
                    pool.wait_ge(x_turned, 2 * i + p - 1)
                pool.wait_ge(ids_loaded[p], 16 * (i + 1))
                pool.sem_inc(gathers_begun, 1)
                for f in range(FIELDS):
                    pool.indirect_dma_start(
                        out=x_rows[p][:, f * DIM:(f + 1) * DIM], out_offset=None,
                        in_=tables[f], in_offset=bass.IndirectOffsetOnAxis(ap=ids_sb[p][:, f:f + 1], axis=0),
                    ).then_inc(gathered[p], 16)

            for p in range(2):
                gather(0, p, True)
            with pool.Fori(1, ROUNDS) as i:
                for p in range(2):
                    gather(i, p, False)

        @block.vector
        def _(dve):
            def turn(i, p):
                dve.wait_ge(gathered[p], 16 * FIELDS * (i + 1))
                nc.vector.transpose(x_gd[p][:, 0:FIELDS, :].rearrange("p f l -> p (f l)"),
                                    x_rows[p][:]).then_inc(x_turned, 1)

            def rest(n, p, blocks=ALL):
                dve.wait_ge(high_ready, n)
                nc.vector.tensor_tensor(x_rest[:, blocks, :],
                                        x_gd[p][:, 0:FIELDS, blocks].rearrange("p f l -> p l f"),
                                        x_parts[:, blocks, 0, :], ALU.subtract).then_inc(rest_ready, 1)

            def low(n, blocks=ALL):
                dve.wait_ge(mid_ready, n)
                nc.vector.tensor_tensor(x_parts[:, blocks, 2, :], x_rest[:, blocks, :],
                                        x_parts[:, blocks, 1, :], ALU.subtract).then_inc(parts_ready, 1)

            def start(t):
                for n, blocks in enumerate((AHEAD, OTHERS)):
                    rest(2 * t + n + 1, t, blocks)
                    low(2 * t + n + 1, blocks)

            def round_(i, first=False, last=False):
                quarter = Count(2 * QUARTERS * i)
                prod = Count(2 * QUARTERS * CHUNKS * i)
                for p in range(2):
                    more = not (last and p == 1 or first and p == 0)
                    i_next, p_next = (i, 1) if p == 0 else (i + 1, 0)
                    t_next = 2 * i + p + 1
                    for q in range(QUARTERS):
                        for step, c in enumerate(ORDER):
                            rows = product_rows(c)
                            if step == 0:
                                dve.wait_ge(left_copied, quarter.value() + 1)
                            if is_shifted(c):
                                dve.wait_ge(shifted[c], (quarter.value() + 1) * (16 * rows // FIELDS))
                                right = product[c][0:rows, :]
                            else:
                                dve.wait_ge(selected, quarter.value() * USES + c + 2)
                                if not (first and (p, q) == (0, 0)):
                                    dve.wait_ge(summed, prod.value() + 1 - CHUNKS)
                                right = selected_ps[c % 2][0:rows, :]
                            prod.next()
                            nc.vector.tensor_tensor(product[c][0:rows, :], left[q % 2][0:rows, :],
                                                    right, ALU.mult).then_inc(products, 1)
                            if first and p == 0 and (q, step) == TURN_SECOND:
                                turn(0, 1)
                            if more and (q, step) == PREPARE["turn"]:
                                dve.wait_ge(spread, t_next - 1)
                                turn(i_next, p_next)
                            if more and (q, step) == PREPARE["rest"]:
                                rest(t_next + 1 + STARTED, p_next)
                            if more and (q, step) == PREPARE["low"]:
                                low(t_next + 1 + STARTED)
                        quarter.next()
                    if first and p == 0:
                        start(1)

            for p in range(2):
                nc.vector.memset(x_gd[p][:, FIELDS:PADDED, :], 0.0).then_inc(cleared, 1)
            nc.vector.memset(hx[:, :, HID + FIELDS:2 * HID], 0.0).then_inc(cleared, 1)
            nc.vector.memset(x_diag[:].rearrange("p l a g f -> p (l a g f)"), 0.0).then_inc(cleared, 1)
            nc.vector.memset(y_sb[:], 0.0).then_inc(y_free, 1)
            dve.wait_ge(consts, 16 * len(CONSTS))
            nc.vector.tensor_tensor(w_pair[:], w_pair[:], w_mirror, ALU.add).then_inc(weights_ready, 1)
            turn(0, 0)
            start(0)
            round_(0, first=True)
            with dve.Fori(1, ROUNDS - 1) as i:
                round_(i)
            round_(ROUNDS - 1, last=True)

        @block.scalar
        def _(act):
            def copy(out, in_):
                return nc.scalar.activation(out, in_, ACT.Copy)

            def high(t, p, blocks=ALL):
                act.wait_ge(x_turned, t + 1)
                copy(x_parts[:, blocks, 0, :], x_gd[p][:, 0:FIELDS, blocks].rearrange("p f l -> p l f"))\
                    .then_inc(high_ready, 1)

            def mid(n, blocks=ALL):
                act.wait_ge(rest_ready, n)
                copy(x_parts[:, blocks, 1, :], x_rest[:, blocks, :]).then_inc(mid_ready, 1)

            def spread_x(p, part):
                if part == 0:
                    copy(hx[:, :, HID:HID + FIELDS], x_gd[p][:, 0:FIELDS, :].rearrange("p f l -> p l f"))
                    return
                rows = slice(DIM * (part - 1), DIM * part)
                last = copy(x_diag[rows, :, :, part - 1, :],
                            x_gd[p][rows, :, :].rearrange("p (f a) l -> p l a f", a=2))
                if part == GROUPS:
                    last.then_inc(spread, 1)

            def take_left(n_quarter, q):
                act.wait_ge(selected, n_quarter * USES + 1)
                copy(left[q % 2][:], selected_ps[1][0:ROWS, :]).then_inc(left_copied, 1)

            def take_hidden(n_summed, q):
                act.wait_ge(summed, n_summed)
                copy(hidden[q % 2][:], hidden_ps[q % 2][:]).then_inc(hidden_copied, 1)

            def aux(counts, work):
                n = counts.next()
                act.wait_ge(aux_ready, counts.value())
                work(aux_ps[(n - 1) % 2]).then_inc(aux_copied, 1)

            def x_turn(counts, p, q):
                aux(counts, lambda bank: copy(x_cols[p][:, q, :], bank[:].bitcast(BF16)[0:ROWS, :]))

            def hidden_turn(counts, q):
                out = hx[:, q * QBLOCKS:(q + 1) * QBLOCKS, 0:HID].rearrange("p (c m) k -> p m c k", c=2)
                aux(counts, lambda bank: copy(out, bank[:].rearrange("p (m c k) -> p m c k", c=2, k=HID)))

            def grams(counts, p, q, b):
                n = GRAM_BATCHES[b]
                l0 = q * QBLOCKS + sum(GRAM_BATCHES[:b])

                def work(bank):
                    view = bank[:, 0:n * GCOLS].rearrange("p (l a g f) -> p a l g f", a=2, g=GROUPS, f=HALF_F)
                    for to, rows in ((gram_h, 0), (gram_x, HID)):
                        cols = to[:, :, TILE * p:TILE * (p + 1)].rearrange("p f (g l) -> p l g f", g=GROUPS)
                        for a in range(2):
                            last = copy(cols[HID * a:HID * (a + 1), l0:l0 + n, :, :],
                                        view[rows:rows + HID, a, :, :, :])
                    return last

                aux(counts, work)

            def round_end(counts, what, i):
                def relu(out, bank, m0, bias, ms):
                    for k in range(ms):
                        last = nc.scalar.activation(out[:, m0 + k, :], bank[:, k * PAIR:(k + 1) * PAIR],
                                                    ACT.Relu, bias=bias[:, m0 + k:m0 + k + 1])
                    return last

                if what == "z":
                    aux(counts, lambda bank: copy(z2[:], bank[:, 0:PAIR]))
                    aux(counts, lambda bank: copy(z1[:], bank[:, 0:PAIR]))
                elif what == "top1":
                    aux(counts, lambda bank: relu(top1, bank, 0, bias1, 2))
                    aux(counts, lambda bank: relu(top1, bank, 2, bias1, 2))
                elif what == "top2":
                    aux(counts, lambda bank: relu(top2, bank, 0, bias2, 2))
                else:
                    act.wait_ge(y_free, i)
                    aux(counts, lambda bank: copy(y_sb[:], bank[0:1, 0:PAIR]))

            def quarter_end(counts, p, q):
                hidden_turn(counts, q)
                for b in range(len(GRAM_BATCHES)):
                    grams(counts, p, q, b)

            def start_high(t):
                for blocks in (AHEAD, OTHERS):
                    high(t, t, blocks)

            def start(counts, t):
                for n, blocks in enumerate((AHEAD, OTHERS)):
                    mid(2 * t + n + 1, blocks)
                for q in range(QUARTERS):
                    x_turn(counts, t, q)
                    if q == 0:
                        take_left(QUARTERS * t, 0)

            def round_(i, first=False, last=False):
                quarter = Count(2 * QUARTERS * i)
                aux_n = Count(QUARTERS if first else aux_start(i))
                for p in range(2):
                    more = not (last and p == 1 or first and p == 0)
                    p_next = 1 - p
                    t = 2 * i + p
                    for q in range(QUARTERS):
                        before = (p, q - 1) if q else (1 - p, QUARTERS - 1)
                        has_before = not (first and (p, q) == (0, 0))
                        end_of_round = not first and (p, q) == (0, 1)
                        for step in range(CHUNKS):
                            if step == 0 and has_before:
                                take_hidden(quarter.value() * CHUNKS, before[1])
                            if step == LEFT_AT and (more or q < QUARTERS - 1):
                                take_left(quarter.value() + 1, q + 1)
                            if q == 1:
                                for part in SPREAD_AT[end_of_round].get(step, ()):
                                    spread_x(p, part)
                            if step == 0 and end_of_round:
                                round_end(aux_n, "z", i)
                            if more and (q, step) in COLS_AT:
                                x_turn(aux_n, p_next, COLS_AT[q, step])
                            if step == 2 and has_before:
                                hidden_turn(aux_n, before[1])
                            if step == 2 and end_of_round:
                                round_end(aux_n, "top1", i)
                            if first and p == 0 and (q, step) == TURN_SECOND:
                                start_high(1)
                            if more and (q, step) == PREPARE["high"]:
                                high(t + 1, p_next)
                            if has_before and step in GRAM_AT:
                                grams(aux_n, *before, GRAM_AT.index(step))
                            if end_of_round and step == 5:
                                round_end(aux_n, "top2", i)
                            if end_of_round and step == 6:
                                round_end(aux_n, "y", i)
                            if more and (q, step) == PREPARE["mid"]:
                                mid(t + 2 + STARTED)
                        quarter.next()
                    if first and p == 0:
                        start(aux_n, 1)
                return aux_n

            act.wait_ge(cleared, 4)
            act.wait_ge(consts, 16 * len(CONSTS))
            copy(select[:], select_f).then_inc(cast, 1)
            copy(eye_bf[:], eye_f[:]).then_inc(cast, 1)
            start_high(0)
            start(Count(0), 0)
            round_(0, first=True)
            with act.Fori(1, ROUNDS - 1) as i:
                round_(i)
            aux_n = round_(ROUNDS - 1, last=True)
            take_hidden(2 * QUARTERS * CHUNKS * ROUNDS, QUARTERS - 1)
            quarter_end(aux_n, 1, QUARTERS - 1)
            for step in ("z", "top1", "top2", "y"):
                round_end(aux_n, step, ROUNDS)

        @block.tensor
        def _(pe):
            def aux(counts, work, needs=None):
                n = counts.next()
                least = n - 2 if needs is None else max(n - 2, needs)
                if not isinstance(counts.start, int) or counts.start + least > 0:
                    pe.wait_ge(aux_copied, counts.value(least))
                work(aux_ps[(n - 1) % 2]).then_inc(aux_ready, 1)
                return n

            def x_turn(counts, q, n_ready=None):
                if n_ready is not None:
                    pe.wait_ge(parts_ready, n_ready)

                def work(bank):
                    for m in range(QBLOCKS):
                        last = nc.tensor.transpose(
                            bank[:].bitcast(BF16)[0:ROWS, m * 128:(m + 1) * 128],
                            x_parts[:, q * QBLOCKS + m, :, :].rearrange("p c f -> p (c f)"), eye_bf[:])
                    return last

                aux(counts, work)

            def hidden_turn(counts, n_copied, q):
                pe.wait_ge(hidden_copied, n_copied)

                def work(bank):
                    for m in range(HALF // 128):
                        cols = slice(m * 128, (m + 1) * 128)
                        last = nc.tensor.transpose(bank[:, cols], hidden[q % 2][:, cols], eye_f[:])
                    return last

                return aux(counts, work)

            def grams(counts, turned, n_spread, q, b):
                if b == 0:
                    pe.wait_ge(spread, n_spread)
                l0 = q * QBLOCKS + sum(GRAM_BATCHES[:b])

                def work(bank):
                    for m in range(GRAM_BATCHES[b]):
                        last = nc.tensor.matmul(
                            bank[:, m * GCOLS:(m + 1) * GCOLS], hx[:, l0 + m, :],
                            x_diag[:, l0 + m, :, :, :].rearrange("p a g f -> p (a g f)"),
                            start=True, stop=True)
                    return last

                return aux(counts, work, turned)

            def z_step(counts, needs):
                def second(bank):
                    for f in range(HALF_F):
                        last = nc.tensor.matmul(bank[:, 0:PAIR], w_second[:, f, :], gram_h[:, f, :],
                                                start=f == 0, stop=f == HALF_F - 1)
                    return last

                def first_(bank):
                    for f in range(HALF_F):
                        half = f % 2
                        last = nc.tensor.matmul(bank[HID * half:HID * (half + 1), 0:PAIR],
                                                w_final[:, f, :], gram_x[:, f, :],
                                                start=f < 2, stop=f >= HALF_F - 2)
                    return last

                aux(counts, second, needs)
                return aux(counts, first_, needs)

            def top1_step(counts, needs, i):
                pe.wait_ge(ctx_loaded, 16 * i)
                for h in range(2):
                    def work(bank):
                        for k in range(2):
                            cols = slice((2 * h + k) * 128, (2 * h + k + 1) * 128)
                            out = bank[:, k * PAIR:(k + 1) * PAIR]
                            nc.tensor.matmul(out, wt1_z1[:, cols], z1[:], start=True, stop=False)
                            nc.tensor.matmul(out, wt1_z2[:, cols], z2[:], start=False, stop=False)
                            last = nc.tensor.matmul(out, wt1_ctx[:, cols], ctx_t[:], start=False, stop=True)
                        return last
                    n = aux(counts, work, needs)
                return n

            def top2_step(counts, needs):
                def work(bank):
                    for k in range(M2):
                        out = bank[:, k * PAIR:(k + 1) * PAIR]
                        for m in range(M1):
                            last = nc.tensor.matmul(out, wt2[:, m, k * 128:(k + 1) * 128], top1[:, m, :],
                                                    start=m == 0, stop=m == M1 - 1)
                    return last
                return aux(counts, work, needs)

            def y_step(counts, needs):
                def work(bank):
                    for m in range(M2):
                        last = nc.tensor.matmul(bank[0:1, 0:PAIR], wt3[:, m:m + 1], top2[:, m, :],
                                                start=m == 0, stop=m == M2 - 1)
                    return last
                aux(counts, work, needs)

            def select_into(bank, what, p, q):
                chunk = 0 if what == "left" else 1 + what
                for h in range(2):
                    last = nc.tensor.matmul(selected_ps[bank][:, h * HALF:(h + 1) * HALF],
                                            select[:, chunk, :], x_cols[p][:, q, h * HALF:(h + 1) * HALF],
                                            start=True, stop=True)
                last.then_inc(selected, 1)

            def sum_products(chunk, q):
                rows = product_rows(chunk)
                for c in range(2):
                    last = nc.tensor.matmul(hidden_ps[q % 2][HID * c:HID * (c + 1), :],
                                            w_pair[0:rows, chunk, :],
                                            product[chunk][0:rows, c * HALF:(c + 1) * HALF],
                                            start=chunk == ORDER[0], stop=chunk == ORDER[-1])
                last.then_inc(summed, 1)

            def start(counts, t):
                for q in range(QUARTERS):
                    if q < 2:
                        x_turn(counts, q, 2 * t + q + 1)
                    else:
                        x_turn(counts, q)
                    if q == 0:
                        pe.wait_ge(aux_copied, counts.value())
                        if t:
                            pe.wait_ge(products, QUARTERS * CHUNKS)
                        select_into(BANK["left"], "left", t, 0)
                        select_into(BANK[0], 0, t, 0)
                pe.wait_ge(aux_copied, counts.value())
                pe.wait_ge(left_copied, QUARTERS * t + 1)
                select_into(BANK[1], 1, t, 0)

            def round_(i, first=False, last=False):
                quarter = Count(2 * QUARTERS * i)
                prod = Count(2 * QUARTERS * CHUNKS * i)
                aux_n = Count(QUARTERS if first else aux_start(i))
                for p in range(2):
                    more = not (last and p == 1 or first and p == 0)
                    t = 2 * i + p
                    for q in range(QUARTERS):
                        before = (p, q - 1) if q else (1 - p, QUARTERS - 1)
                        has_before = not (first and (p, q) == (0, 0))
                        end_of_round = not first and (p, q) == (0, 1)
                        for step, c in enumerate(ORDER):
                            prod.next()
                            if more and (q, step) in COLS_AT:
                                turned_q = COLS_AT[q, step]
                                x_turn(aux_n, turned_q, None if turned_q else t + 2 + STARTED)
                                if turned_q == 0:
                                    turned_0 = aux_n.n
                            if step in SELECT_AT:
                                what, ahead = SELECT_AT[step]
                                if more or q + ahead < QUARTERS:
                                    if (what, ahead) == (1, 1):
                                        pe.wait_ge(left_copied, quarter.value() + 2)
                                    else:
                                        pe.wait_ge(products, prod.value())
                                    if what == "left" and q == QUARTERS - 1:
                                        pe.wait_ge(aux_copied, aux_n.value(turned_0))
                                    select_into(BANK[what], what, (p + (q + ahead) // QUARTERS) % 2,
                                                (q + ahead) % QUARTERS)
                            pe.wait_ge(products, prod.value())
                            if step == 0 and (not first or p or q >= 2):
                                pe.wait_ge(hidden_copied, quarter.value() - 1)
                            sum_products(c, q)
                            if step == 0 and end_of_round:
                                z_n = z_step(aux_n, gram_n)
                            if step == 2 and has_before:
                                turned_n = hidden_turn(aux_n, quarter.value(), before[1])
                            if step == 2 and end_of_round:
                                top_n = top1_step(aux_n, z_n, i)
                            if has_before and step in GRAM_AT:
                                gram_n = grams(aux_n, turned_n, t + 1 if q else t, before[1], GRAM_AT.index(step))
                            if end_of_round and step == 5:
                                top_n = top2_step(aux_n, top_n)
                            if end_of_round and step == 6:
                                y_step(aux_n, top_n)
                        quarter.next()
                    if first and p == 0:
                        start(aux_n, 1)
                return aux_n

            pe.wait_ge(consts, 16 * len(CONSTS))
            pe.wait_ge(cast, 2)
            pe.wait_ge(cleared, 4)
            pe.wait_ge(weights_ready, 1)
            start(Count(0), 0)
            round_(0, first=True)
            with pe.Fori(1, ROUNDS - 1) as i:
                round_(i)
            aux_n = round_(ROUNDS - 1, last=True)
            turned_n = hidden_turn(aux_n, 2 * QUARTERS * ROUNDS, QUARTERS - 1)
            for b in range(len(GRAM_BATCHES)):
                gram_n = grams(aux_n, turned_n, 2 * ROUNDS, QUARTERS - 1, b)
            z_n = z_step(aux_n, gram_n)
            top_n = top1_step(aux_n, z_n, ROUNDS)
            top_n = top2_step(aux_n, top_n)
            y_step(aux_n, top_n)


def build(nc, a, out):
    dlrm_tower(nc, a["dense_t"], a["ids"], [a[f"tbl_{f}"] for f in range(FIELDS)], a["w1_pairs"],
               a["w1_mirrored"], a["w1_final"], a["w2_pairs"], a["w_top1"], a["b_top1"], a["w_top2"],
               a["b_top2"], a["w_top3"], a["selection"], a["ident"], out)


def lay_out(inputs):
    import numpy as np

    w1 = np.asarray(inputs["L0_rec_W1"]).reshape(FIELDS, FIELDS, 2 * HID)
    w2 = np.asarray(inputs["L0_rec_W2"]).reshape(FIELDS, HID, FIN2)
    i = np.arange(FIELDS)
    pairs = np.zeros((COPIES, FIELDS, CHUNKS, HID), np.float32)
    mirrored = np.zeros((COPIES, FIELDS, CHUNKS, HID), np.float32)
    selection = np.zeros((COPIES, FIELDS, 1 + CHUNKS, 128), np.float32)
    for a in range(COPIES):
        selection[:, i, 0, a * FIELDS + i] = 1.0
        for c in range(CHUNKS):
            shift = COPIES * c + a
            if shift >= SHIFTS:
                continue
            j = (i + shift) % FIELDS
            pairs[a, :, c] = w1[i, j, :HID]
            if shift:
                mirrored[a, :, c] = w1[j, i, :HID]
            selection[:, j, 1 + c, a * FIELDS + i] = 1.0
    final = np.zeros((HALF_F, 2, HID, HID), np.float32)
    second = np.zeros((HALF_F, 2, HID, FIN2), np.float32)
    for f in range(FIELDS):
        final[f // 2, f % 2, :FIELDS] = w1[:, f, HID:]
        second[f // 2, f % 2] = w2[f]
    arrays = {
        "dense_t": np.asarray(inputs["dense_ctx"]).T,
        "ids": np.asarray(inputs["ids"]),
        "w1_pairs": pairs.reshape(ROWS, CHUNKS, HID),
        "w1_mirrored": mirrored.reshape(ROWS, CHUNKS, HID),
        "w1_final": final.transpose(1, 2, 0, 3).reshape(128, HALF_F, HID),
        "w2_pairs": second.transpose(1, 2, 0, 3).reshape(128, HALF_F, FIN2),
        "w_top1": np.asarray(inputs["W_top1"]),
        "b_top1": np.asarray(inputs["b_top1"]).reshape(M1, 128).T,
        "w_top2": np.asarray(inputs["W_top2"]),
        "b_top2": np.asarray(inputs["b_top2"]).reshape(M2, 128).T,
        "w_top3": np.asarray(inputs["W_top3"]).reshape(M2, 128).T,
        "selection": selection.reshape(ROWS, 1 + CHUNKS, 128),
        "ident": np.eye(128, dtype=np.float32),
    }
    for f in range(FIELDS):
        arrays[f"tbl_{f}"] = np.asarray(inputs[f"tbl_{f}"])
    return {k: np.ascontiguousarray(v) for k, v in arrays.items()}


def kernel(**inputs):
    import concourse.bacc as bacc
    from concourse.bass_utils import run_bass_kernel_spmd

    arrays = lay_out(inputs)
    nc = bacc.Bacc("TRN2", target_bir_lowering=False, num_devices=1)
    args = {}
    for name, v in arrays.items():
        args[name] = nc.dram_tensor(f"in_{name}", v.shape, mybir.dt.from_np(v.dtype), kind="ExternalInput").ap()
    out = nc.dram_tensor("y_out", (1, BATCH), F32, kind="ExternalOutput").ap()
    build(nc, args, out)
    r = run_bass_kernel_spmd(nc, [{f"in_{k}": v for k, v in arrays.items()}], core_ids=[0])
    return r.results[0]["y_out"].reshape(BATCH, 1)
```

```python
from contextlib import ExitStack

import concourse.bass as bass
from concourse import mybir

F32 = mybir.dt.float32
BF16 = mybir.dt.bfloat16
I32 = mybir.dt.int32
ALU = mybir.AluOpType
ACT = mybir.ActivationFunctionType

FIELDS = 39
DIM = 32
BATCH = 2048
TILE = 128
GROUPS = 4
BLOCKS = TILE // GROUPS
ROUNDS = BATCH // (2 * TILE)
QUARTERS = 4
QCOLS = TILE * DIM // QUARTERS
QBLOCKS = BLOCKS // QUARTERS
HALF = QCOLS // 2
HID = 64
FIN2 = 128
COPIES = 3
ROWS = COPIES * FIELDS
SHIFTS = (FIELDS + 1) // 2
CHUNKS = -(-SHIFTS // COPIES)
LAST_ROWS = (SHIFTS - COPIES * (CHUNKS - 1)) * FIELDS
HALF_F = (FIELDS + 1) // 2
PADDED = 2 * HALF_F
GCOLS = 2 * GROUPS * HALF_F
GRAM_BATCHES = (2, 3, 3)
SELECTED = 2
TOP1, TOP2, CTX = 512, 256, 16
M1, M2 = TOP1 // 128, TOP2 // 128
PAIR = 2 * TILE
USES = SELECTED + 1
BANK = {"left": 1, 0: 0, 1: 1}
SELECT_AT = {1: "left", 2: 0, 4: 1}
LEFT_AT = 1
PREPARE = {False: {"turn": (1, 5), "high": (1, 5), "rest": (2, 2), "mid": (2, 3), "low": (2, 5)},
           True: {"turn": (2, 1), "high": (2, 1), "rest": (2, 3), "mid": (2, 4), "low": (2, 6)}}
COLS_AT = {False: {(2, 6): 0, (3, 0): 1, (3, 3): 2, (3, 5): 3}, True: {(3, 0): 0, (3, 2): 1, (3, 4): 2, (3, 6): 3}}
TURN_SECOND = (3, 3)
ALL = slice(0, BLOCKS)
AHEAD, OTHERS = slice(0, QBLOCKS), slice(QBLOCKS, BLOCKS)
STARTED = 2
GRAM_AT = (4, 5, 6)
ACT_SPREADS = {False: {0: ("rows",), 1: (0,), 2: (1,)}, True: {0: ("rows", 0, 1)}}
ACT_LAST_GROUP = 1
DVE_SPREADS = {3: 2, 4: 3}
DVE_LAST_GROUP = 3
AUX_ROUND = 2 * (QUARTERS + QUARTERS * (1 + len(GRAM_BATCHES))) + 6
AUX_END = 1 + len(GRAM_BATCHES) + 6
Z1_COPY = 1 + len(GRAM_BATCHES) + 1
Z1_LAST = Z1_COPY - QUARTERS
Y_COPY = 2 * (1 + len(GRAM_BATCHES)) + 6
Y_LAST = AUX_END - QUARTERS
Z1_SUM_AT = 5


class Count:

    def __init__(self, start, n=0):
        self.start, self.n = start, n

    def next(self):
        self.n += 1
        return self.n

    def value(self, n=None):
        return self.start + (self.n if n is None else n)


def aux_start(i):
    return i * AUX_ROUND - (AUX_END - QUARTERS)


def product_rows(chunk):
    return LAST_ROWS if chunk == CHUNKS - 1 else ROWS


def is_shifted(chunk):
    return chunk >= SELECTED


def dlrm_tower(nc, dense_t, ids, tables, w1_pairs, w1_mirrored, w1_final, w2_pairs,
               w_top1, b_top1, w_top2, b_top2, w_top3, selection, ident, y):
    ctx = ExitStack()
    with ctx:
        def sb(name, shape, dt=F32):
            return ctx.enter_context(nc.sbuf_tensor(name, shape, dt))

        def pb(name, shape, dt=F32):
            return ctx.enter_context(nc.psum_tensor(name, shape, dt))

        def sem(name):
            return ctx.enter_context(nc.semaphore(name))

        w_pair = sb("w_pair", [ROWS, CHUNKS, HID])
        w_final = sb("w_final", [128, HALF_F, HID])
        w_second = sb("w_second", [128, HALF_F, FIN2])
        wt1_z1_ctx = sb("wt1_z1_ctx", [HID + CTX, TOP1])
        wt1_z2 = sb("wt1_z2", [128, TOP1])
        wt2 = sb("wt2", [128, M1, TOP2])
        wt3 = sb("wt3", [128, M2])
        bias1 = sb("bias1", [128, M1])
        bias2 = sb("bias2", [128, M2])
        select = sb("select", [ROWS, 1 + CHUNKS, 128], BF16)
        eye_bf = sb("eye_bf", [128, 128], BF16)
        eye_f = sb("eye_f", [128, 128])
        ids_sb = [sb(f"ids_sb{p}", [TILE, FIELDS], I32) for p in range(2)]
        x_rows = [sb(f"x_rows{p}", [TILE, FIELDS * DIM]) for p in range(2)]
        x_gd = [sb(f"x_gd{p}", [128, PADDED, BLOCKS]) for p in range(2)]
        x_rest = sb("x_rest", [128, BLOCKS, FIELDS])
        x_parts = sb("x_parts", [128, BLOCKS, COPIES, FIELDS], BF16)
        x_cols = [sb(f"x_cols{p}", [ROWS, QUARTERS, QCOLS], BF16) for p in range(2)]
        left = [sb(f"left{q}", [ROWS, QCOLS]) for q in range(2)]
        product = [sb(f"product{c}", [ROWS, QCOLS]) for c in range(CHUNKS)]
        select_f = product[CHUNKS - 2][:].rearrange("r (c n) -> r c n", n=128)
        w_mirror = product[CHUNKS - 1][:, 0:CHUNKS * HID].rearrange("r (c k) -> r c k", k=HID)
        hidden = [sb(f"hidden{q}", [128, HALF]) for q in range(2)]
        hx = sb("hx", [128, BLOCKS, 2 * HID])
        x_diag = sb("x_diag", [128, BLOCKS, 2, GROUPS, HALF_F])
        gram_h = sb("gram_h", [128, HALF_F, PAIR])
        gram_x = sb("gram_x", [128, HALF_F, PAIR])
        z1_ctx = sb("z1_ctx", [HID + CTX, PAIR])
        z1_odd = sb("z1_odd", [HID, PAIR])
        z2 = sb("z2", [128, PAIR])
        top1 = sb("top1", [128, M1, PAIR])
        top2 = sb("top2", [128, M2, PAIR])
        y_sb = sb("y_sb", [1, PAIR])

        selected_ps = [pb(f"selected_ps{s}", [128, QCOLS]) for s in range(2)]
        hidden_ps = [pb(f"hidden_ps{q}", [128, HALF]) for q in range(2)]
        aux_ps = [pb(f"aux_ps{n}", [128, HALF]) for n in range(2)]

        gathers_begun = sem("gathers_begun")
        consts = sem("consts_loaded")
        cast = sem("constants_cast")
        ids_loaded = [sem(f"ids_loaded{p}") for p in range(2)]
        gathered = [sem(f"gathered{p}") for p in range(2)]
        ctx_loaded = sem("ctx_loaded")
        z1_summed = sem("z1_summed")
        cleared = sem("buffers_cleared")
        weights_ready = sem("pair_weights_summed")
        x_turned = sem("x_turned")
        high_ready = sem("high_part_ready")
        rest_ready = sem("rest_ready")
        mid_ready = sem("mid_part_ready")
        parts_ready = sem("x_parts_ready")
        spread = sem("x_spread")
        selected = sem("selected")
        left_copied = sem("left_copied")
        shifted = {c: sem(f"chunk{c}_shifted") for c in range(CHUNKS) if is_shifted(c)}
        products = sem("products_ready")
        summed = sem("products_summed")
        hidden_copied = sem("hidden_copied")
        aux_ready = sem("aux_ready")
        aux_copied = sem("aux_copied")
        y_free = sem("y_free")
        y_stored = sem("y_stored")

        CONSTS = [
            (w_pair[:], w1_pairs), (w_mirror, w1_mirrored), (eye_f[:], ident), (select_f, selection),
            (w_final[:], w1_final), (w_second[:], w2_pairs),
            (wt1_z1_ctx[0:HID, :], w_top1[0:HID, :]), (wt1_z1_ctx[HID:, :], w_top1[HID + FIN2:, :]),
            (wt1_z2[:], w_top1[HID:HID + FIN2, :]),
            (wt2[:], w_top2.rearrange("(m p) n -> p m n", p=128)),
            (wt3[:], w_top3), (bias1[:], b_top1), (bias2[:], b_top2),
        ]

        def spread_of(p, group):
            rows = slice(DIM * group, DIM * (group + 1))
            return (x_diag[rows, :, :, group, :], x_gd[p][rows, :, :].rearrange("p (f a) l -> p l a f", a=2))

        block = ctx.enter_context(nc.Block())

        @block.sync
        def _(sp):
            def load_ids(i, p):
                sp.dma_start(ids_sb[p][:], ids[bass.ds((2 * i + p) * TILE, TILE), :])\
                  .then_inc(ids_loaded[p], 16)

            def load_ctx(i):
                sp.dma_start(z1_ctx[HID:, :], dense_t[:, bass.ds(i * PAIR, PAIR)])\
                  .then_inc(ctx_loaded, 16)

            def store_y(i):
                last = isinstance(i, int) and i == ROUNDS
                sp.wait_ge(aux_copied, aux_start(i) + (Y_LAST if last else Y_COPY))
                sp.dma_start(y[:, bass.ds((i - 1) * PAIR, PAIR)], y_sb[:]).then_inc(y_stored, 16)
                sp.wait_ge(y_stored, 16 * i)
                sp.sem_inc(y_free, 1)

            def next_ids(i, p):
                sp.wait_ge(gathered[p], 16 * FIELDS * i)
                load_ids(i, p)

            def shift_right_factors(n_quarter, left_q):
                for c in shifted:
                    if c == SELECTED:
                        sp.wait_ge(left_copied, n_quarter + 1)
                    if isinstance(n_quarter, int) and n_quarter == 0:
                        sp.wait_ge(weights_ready, 1)
                        sp.wait_ge(cast, 2)
                    else:
                        sp.wait_ge(summed, CHUNKS * n_quarter - CHUNKS + c + 1)
                    copies = product_rows(c) // FIELDS
                    for a in range(copies):
                        shift = COPIES * c + a
                        row = shift + (1 - a % 2) * FIELDS
                        sp.dma_start(product[c][a * FIELDS:(a + 1) * FIELDS, :],
                                     left[left_q][row:row + FIELDS, :]).then_inc(shifted[c], 16)

            def round_(i, first=False, last=False):
                for n in range(2 * QUARTERS):
                    if n % QUARTERS == 0 and not last:
                        next_ids(i + 1, n // QUARTERS)
                    if n == 2 and not first:
                        store_y(i)
                        load_ctx(i)
                    if not (last and n == 2 * QUARTERS - 1):
                        shift_right_factors(2 * QUARTERS * i + n + 1, (n + 1) % 2)

            for p in range(2):
                load_ids(0, p)
            for dst, src in CONSTS:
                sp.dma_start(dst, src).then_inc(consts, 16)
            load_ctx(0)
            shift_right_factors(0, 0)
            round_(0, first=True)
            with sp.Fori(1, ROUNDS - 1) as i:
                round_(i)
            round_(ROUNDS - 1, last=True)
            store_y(ROUNDS)

        @block.gpsimd
        def _(pool):
            def gather(i, p, first):
                if not first:
                    pool.wait_ge(x_turned, 2 * i + p - 1)
                pool.wait_ge(ids_loaded[p], 16 * (i + 1))
                pool.sem_inc(gathers_begun, 1)
                for f in range(FIELDS):
                    pool.indirect_dma_start(
                        out=x_rows[p][:, f * DIM:(f + 1) * DIM], out_offset=None,
                        in_=tables[f], in_offset=bass.IndirectOffsetOnAxis(ap=ids_sb[p][:, f:f + 1], axis=0),
                    ).then_inc(gathered[p], 16)

            for p in range(2):
                gather(0, p, True)
            with pool.Fori(1, ROUNDS) as i:
                for p in range(2):
                    gather(i, p, False)

        @block.vector
        def _(dve):
            def turn(i, p):
                dve.wait_ge(gathered[p], 16 * FIELDS * (i + 1))
                nc.vector.transpose(x_gd[p][:, 0:FIELDS, :].rearrange("p f l -> p (f l)"),
                                    x_rows[p][:]).then_inc(x_turned, 1)

            def rest(n, p, blocks=ALL):
                dve.wait_ge(high_ready, n)
                nc.vector.tensor_tensor(x_rest[:, blocks, :],
                                        x_gd[p][:, 0:FIELDS, blocks].rearrange("p f l -> p l f"),
                                        x_parts[:, blocks, 0, :], ALU.subtract).then_inc(rest_ready, 1)

            def low(n, blocks=ALL):
                dve.wait_ge(mid_ready, n)
                nc.vector.tensor_tensor(x_parts[:, blocks, 2, :], x_rest[:, blocks, :],
                                        x_parts[:, blocks, 1, :], ALU.subtract).then_inc(parts_ready, 1)

            def start(t):
                for n, blocks in enumerate((AHEAD, OTHERS)):
                    rest(2 * t + n + 1, t, blocks)
                    dve.wait_ge(rest_ready, 2 * t + n + 1)
                    nc.vector.tensor_copy(x_parts[:, blocks, 1, :], x_rest[:, blocks, :]).then_inc(mid_ready, 1)
                    low(2 * t + n + 1, blocks)

            def sum_z1(i, copy_n):
                dve.wait_ge(aux_copied, aux_start(i) + copy_n)
                nc.vector.tensor_tensor(z1_ctx[0:HID, :], z1_ctx[0:HID, :], z1_odd[:], ALU.add)\
                  .then_inc(z1_summed, 1)

            def round_(i, first=False, last=False):
                quarter = Count(2 * QUARTERS * i)
                prod = Count(2 * QUARTERS * CHUNKS * i)
                for p in range(2):
                    more = not (last and p == 1 or first and p == 0)
                    i_next, p_next = (i, 1) if p == 0 else (i + 1, 0)
                    t_next = 2 * i + p + 1
                    for q in range(QUARTERS):
                        for c in range(CHUNKS):
                            rows = product_rows(c)
                            if c == 0:
                                dve.wait_ge(left_copied, quarter.value() + 1)
                            if is_shifted(c):
                                dve.wait_ge(shifted[c], (quarter.value() + 1) * (16 * rows // FIELDS))
                                right = product[c][0:rows, :]
                            else:
                                dve.wait_ge(selected, quarter.value() * USES + c + 2)
                                if not (first and (p, q) == (0, 0)):
                                    dve.wait_ge(summed, prod.value() + 1 - CHUNKS)
                                right = selected_ps[c % 2][0:rows, :]
                            prod.next()
                            nc.vector.tensor_tensor(product[c][0:rows, :], left[q % 2][0:rows, :],
                                                    right, ALU.mult).then_inc(products, 1)
                            if not first and (p, q, c) == (0, 1, Z1_SUM_AT):
                                sum_z1(i, Z1_COPY)
                            if q == 1 and c in DVE_SPREADS:
                                dve.wait_ge(hidden_copied, quarter.value())
                                last_op = nc.vector.tensor_copy(*spread_of(p, DVE_SPREADS[c]))
                                if DVE_SPREADS[c] == DVE_LAST_GROUP:
                                    last_op.then_inc(spread, 1)
                            if first and p == 0 and (q, c) == TURN_SECOND:
                                turn(0, 1)
                            if more and (q, c) == PREPARE[first]["turn"]:
                                dve.wait_ge(spread, 2 * (t_next - 1))
                                turn(i_next, p_next)
                            if more and (q, c) == PREPARE[first]["rest"]:
                                rest(t_next + 1 + STARTED, p_next)
                            if more and (q, c) == PREPARE[first]["low"]:
                                low(t_next + 1 + STARTED)
                        quarter.next()
                    if first and p == 0:
                        start(1)

            for p in range(2):
                nc.vector.memset(x_gd[p][:, FIELDS:PADDED, :], 0.0).then_inc(cleared, 1)
            nc.vector.memset(hx[:, :, HID + FIELDS:2 * HID], 0.0).then_inc(cleared, 1)
            nc.vector.memset(x_diag[:].rearrange("p l a g f -> p (l a g f)"), 0.0).then_inc(cleared, 1)
            nc.vector.memset(y_sb[:], 0.0).then_inc(y_free, 1)
            dve.wait_ge(consts, 16 * len(CONSTS))
            nc.vector.tensor_tensor(w_pair[:], w_pair[:], w_mirror, ALU.add).then_inc(weights_ready, 1)
            turn(0, 0)
            start(0)
            round_(0, first=True)
            with dve.Fori(1, ROUNDS - 1) as i:
                round_(i)
            round_(ROUNDS - 1, last=True)
            sum_z1(ROUNDS, Z1_LAST)

        @block.scalar
        def _(act):
            def copy(out, in_):
                return nc.scalar.activation(out, in_, ACT.Copy)

            def high(t, p, blocks=ALL):
                act.wait_ge(x_turned, t + 1)
                copy(x_parts[:, blocks, 0, :], x_gd[p][:, 0:FIELDS, blocks].rearrange("p f l -> p l f"))\
                    .then_inc(high_ready, 1)

            def mid(n):
                act.wait_ge(rest_ready, n)
                copy(x_parts[:, :, 1, :], x_rest[:]).then_inc(mid_ready, 1)

            def spread_x(p, group):
                if group == "rows":
                    copy(hx[:, :, HID:HID + FIELDS], x_gd[p][:, 0:FIELDS, :].rearrange("p f l -> p l f"))
                    return
                last = copy(*spread_of(p, group))
                if group == ACT_LAST_GROUP:
                    last.then_inc(spread, 1)

            def take_left(n_quarter, q):
                act.wait_ge(selected, n_quarter * USES + 1)
                copy(left[q % 2][:], selected_ps[1][0:ROWS, :]).then_inc(left_copied, 1)

            def take_hidden(n_summed, q):
                act.wait_ge(summed, n_summed)
                copy(hidden[q % 2][:], hidden_ps[q % 2][:]).then_inc(hidden_copied, 1)

            def aux(counts, work):
                n = counts.next()
                act.wait_ge(aux_ready, counts.value())
                work(aux_ps[(n - 1) % 2]).then_inc(aux_copied, 1)

            def x_turn(counts, p, q):
                aux(counts, lambda bank: copy(x_cols[p][:, q, :], bank[:].bitcast(BF16)[0:ROWS, :]))

            def hidden_turn(counts, q):
                out = hx[:, q * QBLOCKS:(q + 1) * QBLOCKS, 0:HID].rearrange("p (c m) k -> p m c k", c=2)
                aux(counts, lambda bank: copy(out, bank[:].rearrange("p (m c k) -> p m c k", c=2, k=HID)))

            def grams(counts, p, q, b):
                n = GRAM_BATCHES[b]
                l0 = q * QBLOCKS + sum(GRAM_BATCHES[:b])

                def work(bank):
                    view = bank[:, 0:n * GCOLS].rearrange("p (l a g f) -> p a l g f", a=2, g=GROUPS, f=HALF_F)
                    for to, rows in ((gram_h, 0), (gram_x, HID)):
                        cols = to[:, :, TILE * p:TILE * (p + 1)].rearrange("p f (g l) -> p l g f", g=GROUPS)
                        for a in range(2):
                            last = copy(cols[HID * a:HID * (a + 1), l0:l0 + n, :, :],
                                        view[rows:rows + HID, a, :, :, :])
                    return last

                aux(counts, work)

            def round_end(counts, what, i):
                def relu(out, bank, m0, bias, ms):
                    for k in range(ms):
                        last = nc.scalar.activation(out[:, m0 + k, :], bank[:, k * PAIR:(k + 1) * PAIR],
                                                    ACT.Relu, bias=bias[:, m0 + k:m0 + k + 1])
                    return last

                if what == "z":
                    def take_z1(bank):
                        copy(z1_ctx[0:HID, :], bank[0:HID, 0:PAIR])
                        return copy(z1_odd[:], bank[HID:2 * HID, 0:PAIR])

                    aux(counts, take_z1)
                    aux(counts, lambda bank: copy(z2[:], bank[:, 0:PAIR]))
                elif what == "top1":
                    aux(counts, lambda bank: relu(top1, bank, 0, bias1, 2))
                    aux(counts, lambda bank: relu(top1, bank, 2, bias1, 2))
                elif what == "top2":
                    aux(counts, lambda bank: relu(top2, bank, 0, bias2, 2))
                else:
                    act.wait_ge(y_free, i)
                    aux(counts, lambda bank: copy(y_sb[:], bank[0:1, 0:PAIR]))

            def quarter_end(counts, p, q):
                hidden_turn(counts, q)
                for b in range(len(GRAM_BATCHES)):
                    grams(counts, p, q, b)

            def start_high(t):
                for blocks in (AHEAD, OTHERS):
                    high(t, t, blocks)

            def start(counts, t):
                for q in range(QUARTERS):
                    x_turn(counts, t, q)
                    if q == 0:
                        take_left(QUARTERS * t, 0)

            def round_(i, first=False, last=False):
                quarter = Count(2 * QUARTERS * i)
                aux_n = Count(QUARTERS if first else aux_start(i))
                for p in range(2):
                    more = not (last and p == 1 or first and p == 0)
                    p_next = 1 - p
                    t = 2 * i + p
                    for q in range(QUARTERS):
                        before = (p, q - 1) if q else (1 - p, QUARTERS - 1)
                        has_before = not (first and (p, q) == (0, 0))
                        end_of_round = not first and (p, q) == (0, 1)
                        for c in range(CHUNKS):
                            if c == 0 and has_before:
                                take_hidden(quarter.value() * CHUNKS, before[1])
                            if c == LEFT_AT and (more or q < QUARTERS - 1):
                                take_left(quarter.value() + 1, q + 1)
                            if q == 1:
                                for group in ACT_SPREADS[end_of_round].get(c, ()):
                                    spread_x(p, group)
                            if c == 0 and end_of_round:
                                round_end(aux_n, "z", i)
                            if more and (q, c) in COLS_AT[first]:
                                x_turn(aux_n, p_next, COLS_AT[first][q, c])
                            if c == 2 and has_before:
                                hidden_turn(aux_n, before[1])
                            if c == 2 and end_of_round:
                                round_end(aux_n, "top1", i)
                            if first and p == 0 and (q, c) == TURN_SECOND:
                                start_high(1)
                            if more and (q, c) == PREPARE[first]["high"]:
                                high(t + 1, p_next)
                            if has_before and c in GRAM_AT:
                                grams(aux_n, *before, GRAM_AT.index(c))
                            if end_of_round and c == 5:
                                round_end(aux_n, "top2", i)
                            if end_of_round and c == 6:
                                round_end(aux_n, "y", i)
                            if more and (q, c) == PREPARE[first]["mid"]:
                                mid(t + 2 + STARTED)
                        quarter.next()
                    if first and p == 0:
                        start(aux_n, 1)
                return aux_n

            act.wait_ge(cleared, 4)
            act.wait_ge(consts, 16 * len(CONSTS))
            copy(select[:], select_f).then_inc(cast, 1)
            copy(eye_bf[:], eye_f[:]).then_inc(cast, 1)
            start_high(0)
            start(Count(0), 0)
            round_(0, first=True)
            with act.Fori(1, ROUNDS - 1) as i:
                round_(i)
            aux_n = round_(ROUNDS - 1, last=True)
            take_hidden(2 * QUARTERS * CHUNKS * ROUNDS, QUARTERS - 1)
            quarter_end(aux_n, 1, QUARTERS - 1)
            for step in ("z", "top1", "top2", "y"):
                round_end(aux_n, step, ROUNDS)

        @block.tensor
        def _(pe):
            def aux(counts, work, needs=None):
                n = counts.next()
                least = n - 2 if needs is None else max(n - 2, needs)
                if not isinstance(counts.start, int) or counts.start + least > 0:
                    pe.wait_ge(aux_copied, counts.value(least))
                work(aux_ps[(n - 1) % 2]).then_inc(aux_ready, 1)
                return n

            def x_turn(counts, q, n_ready=None):
                if n_ready is not None:
                    pe.wait_ge(parts_ready, n_ready)

                def work(bank):
                    for m in range(QBLOCKS):
                        last = nc.tensor.transpose(
                            bank[:].bitcast(BF16)[0:ROWS, m * 128:(m + 1) * 128],
                            x_parts[:, q * QBLOCKS + m, :, :].rearrange("p c f -> p (c f)"), eye_bf[:])
                    return last

                aux(counts, work)

            def hidden_turn(counts, n_copied, q):
                pe.wait_ge(hidden_copied, n_copied)

                def work(bank):
                    for m in range(HALF // 128):
                        cols = slice(m * 128, (m + 1) * 128)
                        last = nc.tensor.transpose(bank[:, cols], hidden[q % 2][:, cols], eye_f[:])
                    return last

                return aux(counts, work)

            def grams(counts, turned, n_spread, q, b):
                if b == 0:
                    pe.wait_ge(spread, 2 * n_spread)
                l0 = q * QBLOCKS + sum(GRAM_BATCHES[:b])

                def work(bank):
                    for m in range(GRAM_BATCHES[b]):
                        last = nc.tensor.matmul(
                            bank[:, m * GCOLS:(m + 1) * GCOLS], hx[:, l0 + m, :],
                            x_diag[:, l0 + m, :, :, :].rearrange("p a g f -> p (a g f)"),
                            start=True, stop=True)
                    return last

                return aux(counts, work, turned)

            def z_step(counts, needs):
                def second(bank):
                    for f in range(HALF_F):
                        last = nc.tensor.matmul(bank[:, 0:PAIR], w_second[:, f, :], gram_h[:, f, :],
                                                start=f == 0, stop=f == HALF_F - 1)
                    return last

                def first_(bank):
                    for f in range(HALF_F):
                        half = f % 2
                        last = nc.tensor.matmul(bank[HID * half:HID * (half + 1), 0:PAIR],
                                                w_final[:, f, :], gram_x[:, f, :],
                                                start=f < 2, stop=f >= HALF_F - 2)
                    return last

                aux(counts, first_, needs)
                return aux(counts, second, needs)

            def top1_step(counts, needs, i):
                pe.wait_ge(ctx_loaded, 16 * i)
                pe.wait_ge(z1_summed, i)
                for h in range(2):
                    def work(bank):
                        for k in range(2):
                            cols = slice((2 * h + k) * 128, (2 * h + k + 1) * 128)
                            out = bank[:, k * PAIR:(k + 1) * PAIR]
                            nc.tensor.matmul(out, wt1_z2[:, cols], z2[:], start=True, stop=False)
                            last = nc.tensor.matmul(out, wt1_z1_ctx[:, cols], z1_ctx[:], start=False, stop=True)
                        return last
                    n = aux(counts, work, needs)
                return n

            def top2_step(counts, needs):
                def work(bank):
                    for k in range(M2):
                        out = bank[:, k * PAIR:(k + 1) * PAIR]
                        for m in range(M1):
                            last = nc.tensor.matmul(out, wt2[:, m, k * 128:(k + 1) * 128], top1[:, m, :],
                                                    start=m == 0, stop=m == M1 - 1)
                    return last
                return aux(counts, work, needs)

            def y_step(counts, needs):
                def work(bank):
                    for m in range(M2):
                        last = nc.tensor.matmul(bank[0:1, 0:PAIR], wt3[:, m:m + 1], top2[:, m, :],
                                                start=m == 0, stop=m == M2 - 1)
                    return last
                aux(counts, work, needs)

            def select_into(bank, what, p, q):
                chunk = 0 if what == "left" else 1 + what
                for h in range(2):
                    last = nc.tensor.matmul(selected_ps[bank][:, h * HALF:(h + 1) * HALF],
                                            select[:, chunk, :], x_cols[p][:, q, h * HALF:(h + 1) * HALF],
                                            start=True, stop=True)
                last.then_inc(selected, 1)

            def sum_products(chunk, q):
                rows = product_rows(chunk)
                for c in range(2):
                    last = nc.tensor.matmul(hidden_ps[q % 2][HID * c:HID * (c + 1), :],
                                            w_pair[0:rows, chunk, :],
                                            product[chunk][0:rows, c * HALF:(c + 1) * HALF],
                                            start=chunk == 0, stop=chunk == CHUNKS - 1)
                last.then_inc(summed, 1)

            def start(counts, t):
                for q in range(QUARTERS):
                    if q < 2:
                        x_turn(counts, q, 2 * t + q + 1)
                    else:
                        x_turn(counts, q)
                    if q == 0:
                        pe.wait_ge(aux_copied, counts.value())
                        if t:
                            pe.wait_ge(products, QUARTERS * CHUNKS)
                        select_into(BANK["left"], "left", t, 0)
                        select_into(BANK[0], 0, t, 0)
                    if q == 1:
                        pe.wait_ge(left_copied, QUARTERS * t + 1)
                        select_into(BANK[1], 1, t, 0)

            def round_(i, first=False, last=False):
                quarter = Count(2 * QUARTERS * i)
                prod = Count(2 * QUARTERS * CHUNKS * i)
                aux_n = Count(QUARTERS if first else aux_start(i))
                for p in range(2):
                    more = not (last and p == 1 or first and p == 0)
                    t = 2 * i + p
                    for q in range(QUARTERS):
                        before = (p, q - 1) if q else (1 - p, QUARTERS - 1)
                        has_before = not (first and (p, q) == (0, 0))
                        end_of_round = not first and (p, q) == (0, 1)
                        for c in range(CHUNKS):
                            prod.next()
                            if more and (q, c) in COLS_AT[first]:
                                turned_q = COLS_AT[first][q, c]
                                x_turn(aux_n, turned_q, None if turned_q else t + 2 + STARTED)
                                if turned_q == 0:
                                    turned_0 = aux_n.n
                            if c in SELECT_AT and (more or q < QUARTERS - 1):
                                what = SELECT_AT[c]
                                if what == "left":
                                    pe.wait_ge(products, prod.value())
                                    if first and q == 0:
                                        pe.wait_ge(aux_copied, aux_n.value())
                                    if q == QUARTERS - 1:
                                        pe.wait_ge(aux_copied, aux_n.value(turned_0))
                                elif what == 1:
                                    pe.wait_ge(left_copied, quarter.value() + 2)
                                select_into(BANK[what], what, (p + (q + 1) // QUARTERS) % 2,
                                            (q + 1) % QUARTERS)
                            pe.wait_ge(products, prod.value())
                            if c == 0 and (not first or p or q >= 2):
                                pe.wait_ge(hidden_copied, quarter.value() - 1)
                            sum_products(c, q)
                            if c == 0 and end_of_round:
                                z_n = z_step(aux_n, gram_n)
                            if c == 2 and has_before:
                                turned_n = hidden_turn(aux_n, quarter.value(), before[1])
                            if c == 2 and end_of_round:
                                top_n = top1_step(aux_n, z_n, i)
                            if has_before and c in GRAM_AT:
                                gram_n = grams(aux_n, turned_n, t + 1 if q else t, before[1], GRAM_AT.index(c))
                            if end_of_round and c == 5:
                                top_n = top2_step(aux_n, top_n)
                            if end_of_round and c == 6:
                                y_step(aux_n, top_n)
                        quarter.next()
                    if first and p == 0:
                        start(aux_n, 1)
                return aux_n

            pe.wait_ge(consts, 16 * len(CONSTS))
            pe.wait_ge(cast, 2)
            pe.wait_ge(cleared, 4)
            pe.wait_ge(weights_ready, 1)
            start(Count(0), 0)
            round_(0, first=True)
            with pe.Fori(1, ROUNDS - 1) as i:
                round_(i)
            aux_n = round_(ROUNDS - 1, last=True)
            turned_n = hidden_turn(aux_n, 2 * QUARTERS * ROUNDS, QUARTERS - 1)
            for b in range(len(GRAM_BATCHES)):
                gram_n = grams(aux_n, turned_n, 2 * ROUNDS, QUARTERS - 1, b)
            z_n = z_step(aux_n, gram_n)
            top_n = top1_step(aux_n, z_n, ROUNDS)
            top_n = top2_step(aux_n, top_n)
            y_step(aux_n, top_n)


def build(nc, a, out):
    dlrm_tower(nc, a["dense_t"], a["ids"], [a[f"tbl_{f}"] for f in range(FIELDS)], a["w1_pairs"],
               a["w1_mirrored"], a["w1_final"], a["w2_pairs"], a["w_top1"], a["b_top1"], a["w_top2"],
               a["b_top2"], a["w_top3"], a["selection"], a["ident"], out)


def lay_out(inputs):
    import numpy as np

    w1 = np.asarray(inputs["L0_rec_W1"]).reshape(FIELDS, FIELDS, 2 * HID)
    w2 = np.asarray(inputs["L0_rec_W2"]).reshape(FIELDS, HID, FIN2)
    i = np.arange(FIELDS)
    pairs = np.zeros((COPIES, FIELDS, CHUNKS, HID), np.float32)
    mirrored = np.zeros((COPIES, FIELDS, CHUNKS, HID), np.float32)
    selection = np.zeros((COPIES, FIELDS, 1 + CHUNKS, 128), np.float32)
    for a in range(COPIES):
        selection[:, i, 0, a * FIELDS + i] = 1.0
        for c in range(CHUNKS):
            shift = COPIES * c + a
            if shift >= SHIFTS:
                continue
            j = (i + shift) % FIELDS
            pairs[a, :, c] = w1[i, j, :HID]
            if shift:
                mirrored[a, :, c] = w1[j, i, :HID]
            selection[:, j, 1 + c, a * FIELDS + i] = 1.0
    final = np.zeros((HALF_F, 2, HID, HID), np.float32)
    second = np.zeros((HALF_F, 2, HID, FIN2), np.float32)
    for f in range(FIELDS):
        final[f // 2, f % 2, :FIELDS] = w1[:, f, HID:]
        second[f // 2, f % 2] = w2[f]
    arrays = {
        "dense_t": np.asarray(inputs["dense_ctx"]).T,
        "ids": np.asarray(inputs["ids"]),
        "w1_pairs": pairs.reshape(ROWS, CHUNKS, HID),
        "w1_mirrored": mirrored.reshape(ROWS, CHUNKS, HID),
        "w1_final": final.transpose(1, 2, 0, 3).reshape(128, HALF_F, HID),
        "w2_pairs": second.transpose(1, 2, 0, 3).reshape(128, HALF_F, FIN2),
        "w_top1": np.asarray(inputs["W_top1"]),
        "b_top1": np.asarray(inputs["b_top1"]).reshape(M1, 128).T,
        "w_top2": np.asarray(inputs["W_top2"]),
        "b_top2": np.asarray(inputs["b_top2"]).reshape(M2, 128).T,
        "w_top3": np.asarray(inputs["W_top3"]).reshape(M2, 128).T,
        "selection": selection.reshape(ROWS, 1 + CHUNKS, 128),
        "ident": np.eye(128, dtype=np.float32),
    }
    for f in range(FIELDS):
        arrays[f"tbl_{f}"] = np.asarray(inputs[f"tbl_{f}"])
    return {k: np.ascontiguousarray(v) for k, v in arrays.items()}


def kernel(**inputs):
    import concourse.bacc as bacc
    from concourse.bass_utils import run_bass_kernel_spmd

    arrays = lay_out(inputs)
    nc = bacc.Bacc("TRN2", target_bir_lowering=False, num_devices=1)
    args = {}
    for name, v in arrays.items():
        args[name] = nc.dram_tensor(f"in_{name}", v.shape, mybir.dt.from_np(v.dtype), kind="ExternalInput").ap()
    out = nc.dram_tensor("y_out", (1, BATCH), F32, kind="ExternalOutput").ap()
    build(nc, args, out)
    r = run_bass_kernel_spmd(nc, [{f"in_{k}": v for k, v in arrays.items()}], core_ids=[0])
    return r.results[0]["y_out"].reshape(BATCH, 1)
```
